# Optimizing a Trainium2 kernel written in Bass

```python
import numpy as np
import jax
import jax.numpy as jnp

def _softmax(x, axis=-1):
    return jax.nn.softmax(x, axis=axis)

def _gelu(x):
    return jax.nn.gelu(x, approximate=True)

def _silu(x):
    return jax.nn.silu(x)

def _sigmoid(x):
    return jax.nn.sigmoid(x)

def _layernorm(x, axis=-1, eps=1e-05):
    m = jnp.mean(x, axis=axis, keepdims=True)
    v = jnp.var(x, axis=axis, keepdims=True)
    return (x - m) / jnp.sqrt(v + eps)

def _scatter_add(tgt, idx, src, axis=0):
    return tgt.at[idx].add(src)

def _segment_sum(src, seg, n):
    return jax.ops.segment_sum(src, seg, n)
kernel_name = 'mk_prb_d1_jaxref_r4_9d34b8'

def setup_inputs(seed: int=0):
    np.random.seed(seed)
    _w = jnp.asarray

    def _L0_attn_setup():
        import jax, jax.numpy as jnp
        import numpy as np
        B, L, C, H, W = (4, 1024, 256, 16, 128)
        D = C // H
        STRIDE = W // 2

        def _local_attention(x, w_qkv, b_qkv, w_out, b_out):
            b, l, c = x.shape
            pad = -l % W
            x = jnp.pad(x, ((0, 0), (0, pad), (0, 0)))
            lp = l + pad
            qkv = (x @ w_qkv + b_qkv).reshape(b, lp, 3, H, D).transpose(2, 0, 3, 1, 4)
            q, k, v = (qkv[0], qkv[1], qkv[2])
            nw = (lp - W) // STRIDE + 1
            idx = jnp.arange(nw)[:, None] * STRIDE + jnp.arange(W)[None, :]
            qw = q[:, :, idx, :]
            kw = k[:, :, idx, :]
            vw = v[:, :, idx, :]
            scores = jnp.einsum('bhnqd,bhnkd->bhnqk', qw, kw) / jnp.sqrt(jnp.float32(D))
            probs = jax.nn.softmax(scores, axis=-1)
            ow = jnp.einsum('bhnqk,bhnkd->bhnqd', probs, vw)
            o = ow.transpose(0, 2, 3, 1, 4).reshape(b, nw * W, c)
            o = o @ w_out + b_out
            return o[:, :l, :]
        key = jax.random.key(seed)
        k0, k1, k2 = jax.random.split(key, 3)
        s = 0.02
        return {'x': jax.random.normal(k0, (B, L, C), jnp.float32), 'w_qkv': jax.random.normal(k1, (C, 3 * C), jnp.float32) * s, 'b_qkv': jnp.zeros((3 * C,), jnp.float32), 'w_out': jax.random.normal(k2, (C, C), jnp.float32) * s, 'b_out': jnp.zeros((C,), jnp.float32)}
    _L0_attn_in = _L0_attn_setup()

    def _L0_ffn_setup():
        import jax, jax.numpy as jnp
        import numpy as np
        TOP_K = 2
        key = jax.random.key(seed)
        k1, k2, k3, k4 = jax.random.split(key, 4)
        B, T, D, H, E = (2, 512, 256, 512, 8)
        x = jax.random.normal(k1, (B, T, D), dtype=jnp.float32)
        w12 = jax.random.normal(k2, (E, 2 * H, D), dtype=jnp.float32) * D ** (-0.5)
        w3 = jax.random.normal(k3, (E, D, H), dtype=jnp.float32) * H ** (-0.5)
        gate_w = jax.random.normal(k4, (E, D), dtype=jnp.float32) * D ** (-0.5)
        return {'x': x, 'w12': w12, 'w3': w3, 'gate_w': gate_w}
    _L0_ffn_in = _L0_ffn_setup()
    _d = {'L0_attn_x': _L0_attn_in['x'], 'L0_attn_w_qkv': _L0_attn_in['w_qkv'], 'L0_attn_b_qkv': _L0_attn_in['b_qkv'], 'L0_attn_w_out': _L0_attn_in['w_out'], 'L0_attn_b_out': _L0_attn_in['b_out'], 'L0_ffn_w12': _L0_ffn_in['w12'], 'L0_ffn_w3': _L0_ffn_in['w3'], 'L0_ffn_gate_w': _L0_ffn_in['gate_w']}
    _x0 = _d['L0_attn_x']
    _d['L0_attn_x'] = jax.random.normal(jax.random.fold_in(jax.random.key(seed), 1), (8, 512, 256), dtype=_x0.dtype)
    del _x0
    return _d

def reference(L0_attn_x, L0_attn_w_qkv, L0_attn_b_qkv, L0_attn_w_out, L0_attn_b_out, L0_ffn_w12, L0_ffn_w3, L0_ffn_gate_w):

    def _L0_attn_ref(x, w_qkv, b_qkv, w_out, b_out):
        import jax, jax.numpy as jnp
        import numpy as np
        B, L, C, H, W = (4, 1024, 256, 16, 128)
        D = C // H
        STRIDE = W // 2

        def _local_attention(x, w_qkv, b_qkv, w_out, b_out):
            b, l, c = x.shape
            pad = -l % W
            x = jnp.pad(x, ((0, 0), (0, pad), (0, 0)))
            lp = l + pad
            qkv = (x @ w_qkv + b_qkv).reshape(b, lp, 3, H, D).transpose(2, 0, 3, 1, 4)
            q, k, v = (qkv[0], qkv[1], qkv[2])
            nw = (lp - W) // STRIDE + 1
            idx = jnp.arange(nw)[:, None] * STRIDE + jnp.arange(W)[None, :]
            qw = q[:, :, idx, :]
            kw = k[:, :, idx, :]
            vw = v[:, :, idx, :]
            scores = jnp.einsum('bhnqd,bhnkd->bhnqk', qw, kw) / jnp.sqrt(jnp.float32(D))
            probs = jax.nn.softmax(scores, axis=-1)
            ow = jnp.einsum('bhnqk,bhnkd->bhnqd', probs, vw)
            o = ow.transpose(0, 2, 3, 1, 4).reshape(b, nw * W, c)
            o = o @ w_out + b_out
            return o[:, :l, :]
        return _local_attention(x, w_qkv, b_qkv, w_out, b_out)

    def _L0_ffn_ref(x, w12, w3, gate_w):
        import jax, jax.numpy as jnp
        import numpy as np
        TOP_K = 2
        E = gate_w.shape[0]
        H = w3.shape[-1]
        scores = jnp.einsum('btd,ed->bte', x, gate_w)
        topk_scores, topk_idx = jax.lax.top_k(scores, TOP_K)
        topk_probs = jax.nn.softmax(topk_scores, axis=-1)
        total_probs = jnp.sum(jax.nn.one_hot(topk_idx, E, dtype=topk_probs.dtype) * topk_probs[..., None], axis=-2)
        h12 = jnp.einsum('btd,ehd->bteh', x, w12)
        h1, h2 = (h12[..., :H], h12[..., H:])
        hidden = jax.nn.silu(h1) * h2
        expert_out = jnp.einsum('bteh,edh->bted', hidden, w3)
        y = jnp.sum(total_probs[..., None] * expert_out, axis=-2)
        return y
    x = L0_attn_x
    xn = _layernorm(x, axis=-1)
    x = x + _L0_attn_ref(xn, L0_attn_w_qkv, L0_attn_b_qkv, L0_attn_w_out, L0_attn_b_out) + _L0_ffn_ref(xn, L0_ffn_w12, L0_ffn_w3, L0_ffn_gate_w)
    return x

_drawn_inputs = setup_inputs


def setup_inputs(seed=0):
    import zlib

    import numpy as np

    out = dict(_drawn_inputs(seed))
    spreads = {'L0_attn_b_qkv': (0.0, 0.285), 'L0_attn_b_out': (0.0, 0.1)}
    factors = {'L0_attn_w_qkv': 7.014}
    for name, (base, spread) in spreads.items():
        noise = np.random.default_rng([zlib.crc32(name.encode()), seed]).standard_normal(out[name].shape)
        drawn = base * np.exp(spread * noise) if base else spread * noise
        out[name] = jnp.asarray(drawn.astype(out[name].dtype))
    for name, factor in factors.items():
        out[name] = (out[name] * factor).astype(out[name].dtype)
    return out
```

```python
from contextlib import ExitStack, contextmanager

import concourse.bass as bass
from concourse import mybir

F32 = mybir.dt.float32
BF16 = mybir.dt.bfloat16
I32 = mybir.dt.int32
U32 = mybir.dt.uint32
ALU = mybir.AluOpType
ACT = mybir.ActivationFunctionType
AX_X = mybir.AxisListType.X

P = 128
B, L, D = 8, 512, 256
NC_D = D // P
TB = L // P
NT = B * TB
H, HD = 16, 16
WIN, STRIDE = 128, 64
NWIN = L // WIN
SPAN = STRIDE * (NWIN - 1) + WIN
HH = H // 2
UNITS = 2 * NWIN
HQ = HH // 2
SCALE = float(HD) ** -0.5
E, FH = 8, 512
FC = FH // P
SLOT_TILES = (2 * B * L + E * (P - 1)) // P
XS_TILES = SLOT_TILES + 1
WE = NC_D * 2 * FH + FC * D
EPS = 1e-5
BANK = 512
FAR = -3.0e38
Q_LEVELS = (0, 0, 1, 0, 2, 1)
K_LEVELS = (0, 1, 0, 2, 0, 1)
NLEV = len(Q_LEVELS)
STK = NLEV * HD
NPART = 3
PAIRS = 2


class Count:

    def __init__(self, start=0, per=0):
        self.base, self.n, self.per = start, 0, per

    def add(self, k=1):
        self.n += k
        return self.base + self.n

    def now(self, less=0):
        return self.base + (self.n - less)


@contextmanager
def loop(eng, times, *counts):
    starts = [c.now() for c in counts]
    with eng.Fori(0, times) as i:
        for c, s in zip(counts, starts):
            c.base, c.n = i * c.per + s, 0
        yield i
        for c in counts:
            assert c.n == c.per, (c.n, c.per)
    for c, s in zip(counts, starts):
        c.base, c.n = s + times * c.per, 0


def wait_some(eng, sem, value):
    if not (isinstance(value, int) and value == 0):
        eng.wait_ge(sem, value)


def layer(nc, x, wqkv, bqk, bv, wout, bout, gate, wexp, out):
    with ExitStack() as ctx:
        def sb(name, shape, dt=F32):
            return ctx.enter_context(nc.sbuf_tensor(name, shape, dt))

        def sem(name):
            return ctx.enter_context(nc.semaphore(name))

        xs_dram = nc.dram_tensor("xs_scratch", (XS_TILES * P, D), F32, kind="Internal").ap()
        ys_dram = nc.dram_tensor("ys_scratch", (SLOT_TILES * P, D), F32, kind="Internal").ap()
        pd_dram = nc.dram_tensor("parts_scratch", (B + 1, NPART, 2, H, HD, SPAN), BF16, kind="Internal").ap()
        xt_dram = nc.dram_tensor("xt_scratch", (B + 1, P, NC_D, SPAN), F32, kind="Internal").ap()

        XN = sb("XN", [P, NT, D])
        WALL = sb("WALL", [P, E * WE])
        QS = sb("QS", [STK, 2, H, SPAN], BF16)
        KS = sb("KS", [STK, 2, H, SPAN], BF16)
        WORK = sb("WORK", [P, 4928])
        VW = sb("VW", [P, NWIN, H, HD + 1])
        WQKV = sb("WQKV", [P, NC_D, 3 * D])
        WOUT = sb("WOUT", [P, NC_D, D])
        BOUT = sb("BOUT", [P, D])
        BQK = sb("BQK", [P, 4])
        IDF = sb("IDF", [P, P])
        IDB = sb("IDB", [P, P], BF16)
        SEL = sb("SEL", [STK, HH, P], BF16)
        OSB = sb("OSB", [P, H, HD])
        OTS = sb("OTS", [P, NC_D, P])
        MNEG = sb("MNEG", [P, HH])
        MH = sb("MH", [P, STK], BF16)
        NEGM = sb("NEGM", [STK, 2, P], BF16)
        RDEN = sb("RDEN", [P, H])
        PW = sb("PW", [P, 2, NT])
        IDX = sb("IDX", [P, 2, NT], U32)
        EJ = sb("EJ", [1, XS_TILES], I32)

        nq = 4 * SPAN // 2
        PARTS = WORK[:, 0:NPART * nq].bitcast(BF16).rearrange("p (l k t) -> p l k t", l=NPART, k=4)
        at = NPART * nq
        REST = WORK[:, at:at + SPAN]
        at += SPAN
        XNT = WORK[:, at:at + NC_D * SPAN].rearrange("p (c t) -> p c t", c=NC_D)
        at += NC_D * SPAN
        PT = WORK[:, at:at + 4 * BANK].rearrange("p (r n) -> p r n", r=4)
        assert at + 4 * BANK <= 4928
        at = 0

        def work(n):
            nonlocal at
            at += n
            assert at <= 4928
            return WORK[:, at - n:at]

        XS = work(2 * D).rearrange("p (b n) -> p b n", b=2)
        XTS = work(2 * D).rearrange("p (b c n) -> p b c n", b=2, c=NC_D)
        HID = work(2 * FH).rearrange("p (b n) -> p b n", b=2)
        HTS = work(FH).rearrange("p (c n) -> p c n", c=FC)
        YS = work(2 * D).rearrange("p (b n) -> p b n", b=2)
        at = 0

        def temp(n, dt=F32):
            nonlocal at
            at += n
            assert at <= E * WE
            v = WALL[:, at - n:at]
            return v if dt == F32 else v.bitcast(dt)

        ZERO = temp(XS_TILES * P * D // P // 4)
        XT = temp(NC_D * NT * P).rearrange("p (c n) -> p c n", c=NC_D)
        GW = temp(NC_D * E).rearrange("p (c e) -> p c e", c=NC_D)
        BV = temp(NC_D)
        BVB = temp(NC_D * P).rearrange("p (c n) -> p c n", c=NC_D)
        BEFORE = temp(P)
        ONES = temp(P)
        STAT = temp(NT * 6).rearrange("p (t s) -> p t s", s=6)
        MEAN, VAR, DIF, STD, RS, TMP = (temp(NT) for _ in range(6))
        G, EQ, KEY, OH1, G2, OH2, MASK, RANK, SLOT, PICK = (
            temp(NT * E).rearrange("p (t e) -> p t e", e=E) for _ in range(10))
        TOT, INC, EXC, RMASK = (temp(NT * E) for _ in range(4))
        M1, KM, M2, E2, PA = (temp(NT) for _ in range(5))
        REV, NTL, INCT, BASE = (temp(E) for _ in range(4))
        ONE8 = temp(E)
        TH = temp(NT)
        CMP = temp(E * NT).rearrange("p (e t) -> p e t", e=E)
        JI = temp(XS_TILES)
        CMPJ = temp(XS_TILES * E).rearrange("p (j e) -> p j e", e=E)
        EJF = temp(XS_TILES)
        INTS = temp(E + NT + XS_TILES, I32)
        SLOTF = temp(2 * NT).rearrange("p (k t) -> p k t", k=2)
        assert 2 * NT * D + NT * D == E * WE
        YG = WALL[:, 0:2 * NT * D].rearrange("p (t k d) -> p t k d", k=2, d=D)
        XR = WALL[:, 2 * NT * D:].rearrange("p (t d) -> p t d", d=D)

        PS = ctx.enter_context(nc.psum_tensor("PS", [P, 8 * BANK], F32))

        def bank(k, n=1):
            return PS[:, k * BANK:(k + n) * BANK]

        S_BANKS = bank(0, 2)
        ST_BANK = (bank(2), bank(3))
        O_BANK, T_BANK, W_BANK, R_BANK = bank(4), bank(5), bank(6), bank(7)

        x_in = [sem(f"x_in{g}") for g in range(4)]
        consts_in = sem("consts_in")
        consts_made = sem("consts_made")
        zero_made = sem("zero_made")
        xs_zeroed = sem("xs_zeroed")
        var_ready = sem("var_ready")
        std_ready = sem("std_ready")
        xn_ready = sem("xn_ready")
        gates_full = sem("gates_full")
        xt_out = sem("xt_out")
        xnt_in = sem("xnt_in")
        bv_ready = sem("bv_ready")
        mask_ready = sem("mask_ready")
        ranks_full = sem("ranks_full")
        gap_ready = sem("gap_ready")
        e2_ready = sem("e2_ready")
        slots_ready = sem("slots_ready")
        scattered = [sem(f"scattered{b}") for b in range(B)]
        xn_taken = sem("xn_taken")
        scatter_done = sem("scatter_done")
        t_full, t_free = sem("t_full"), sem("t_free")
        w_full, w_free = sem("w_full"), sem("w_free")
        s_full, s_free = sem("s_full"), sem("s_free")
        mh_ready = sem("mh_ready")
        st_full, probs_ready = sem("st_full"), sem("probs_ready")
        o_full, o_free = sem("o_full"), sem("o_free")
        r_full, r_free = sem("r_full"), sem("r_free")
        part0_ready = sem("part0_ready")
        parts_ready = sem("parts_ready")
        parts_out = sem("parts_out")
        stack_in = [sem("stack_in0"), sem("stack_in1")]
        weights_in = sem("weights_in")
        phase_done = sem("phase_done")
        xs_in = [sem("xs_in0"), sem("xs_in1")]
        xt_full, xt_free = sem("xt_full"), sem("xt_free")
        h1_full, tanh_ready, g_done = sem("h1_full"), sem("tanh_ready"), sem("g_done")
        h2_full, hid_done = sem("h2_full"), sem("hid_done")
        ht_full, ht_free = sem("ht_full"), sem("ht_free")
        y_full, ys_ready = sem("y_full"), sem("ys_ready")
        y_out = [sem("y_out0"), sem("y_out1")]
        gathered = [sem(f"gathered{b}") for b in range(B // 2)]
        rows_back = sem("rows_back")
        xr_in = sem("xr_in")
        sum_done = sem("sum_done")
        out_done = sem("out_done")
        dve_step = sem("dve_step")

        block = ctx.enter_context(nc.Block())

        def pair_counts():
            return dict(T=Count(0, 2 * (UNITS + NWIN)), W=Count(0, 2 * 8), S=Count(0, 2 * UNITS),
                        ST=Count(0, 4 * UNITS), O=Count(0, 2 * NWIN), R=Count(0, 2 * NWIN),
                        NB=Count(0, 2), QK=Count(0, 8))

        CONSTS = 17
        PAIR_STEPS = (2 * (UNITS + NWIN + 4), 2 * (UNITS + NWIN + 4 + 4 * NWIN))

        @block.sync
        def _(sp):
            xv = x.rearrange("(t p) d -> p t d", p=P)
            for g in range(4):
                sp.dma_start(XN[:, 8 * g:8 * g + 8, :], xv[:, 8 * g:8 * g + 8, :]).then_inc(x_in[g], 16)
            sp.wait_ge(zero_made, 1)
            zv = xs_dram.rearrange("(p r) d -> p (r d)", p=P)
            q = XS_TILES * D // 4
            for g in range(4):
                sp.dma_start(zv[:, g * q:(g + 1) * q], ZERO).then_inc(xs_zeroed, 16)

            for nb in range(B + 1):
                src = nb % B
                sp.wait_ge(t_free, (src + 1) * TB // 2)
                sp.wait_ge(w_free, (src + 1) * TB // 2)
                sp.dma_start(xt_dram[nb], XT[:, :, src * L:src * L + SPAN]).then_inc(xt_out, 16)

            PARTS_OUT = 2 * NPART * 16

            def stacks(nb, par):
                def of(l, k):
                    return pd_dram[bass.ds(nb, 1), l, k].rearrange("o h d t -> (o h) d t")

                sp.wait_ge(parts_ready, nb * 4 + 4)
                for l in range(NPART):
                    for k in range(2):
                        sp.dma_start(of(l, k).rearrange("(b h) d t -> (h d) b t", b=2),
                                     PARTS[:, l, 2 * k:2 * k + 2, :]).then_inc(parts_out, 16)
                sp.wait_ge(parts_out, nb * PARTS_OUT + PARTS_OUT)
                for l in range(NLEV):
                    for k, (stack, lev) in enumerate(((QS, Q_LEVELS), (KS, K_LEVELS))):
                        sp.dma_start(stack[HD * l:HD * l + HD, par], of(lev[l], k).rearrange("h d t -> d h t")
                                     ).then_inc(stack_in[par], 16)

            stacks(0, 0)
            sp.wait_ge(xt_out, 16 * (B + 1))
            for stage in range(2):
                with sp.Fori(0, PAIRS) as i:
                    for par in range(2):
                        b = 2 * i + (4 * stage + par)
                        sp.wait_ge(w_full, b * 8 + (NT // 2 + 8))
                        sp.dma_start(XNT, xt_dram[bass.ds(b + 1, 1)].rearrange("o p c t -> (o p) c t")
                                     ).then_inc(xnt_in, 16)
                        sp.wait_ge(r_free, b * NWIN + 2)
                        if stage == 0:
                            sp.wait_ge(xs_zeroed, 64)
                            sp.dma_start(WALL[:, bass.ds(b * (2 * WE), WE)], wexp[:, bass.ds(b * (2 * WE), WE)]
                                         ).then_inc(weights_in, 16)
                        stacks(b + 1, 1 - par)
                        if stage == 0:
                            sp.dma_start(WALL[:, bass.ds(b * (2 * WE) + WE, WE)], wexp[:, bass.ds(b * (2 * WE) + WE, WE)]
                                         ).then_inc(weights_in, 16)
                if stage:
                    break
                sp.wait_ge(scatter_done, 1)
                sp.wait_ge(phase_done, 3)
                for j in range(2):
                    sp.dma_start(XS[:, j, :], xs_dram[j * P:(j + 1) * P, :]).then_inc(xs_in[j], 16)
                with sp.Fori(0, SLOT_TILES // 2) as i:
                    for j in range(2):
                        sp.wait_ge(xt_full, 2 * i + (j + 1))
                        sp.dma_start(XS[:, j, :], xs_dram[bass.ds(i * (2 * P) + (j + 2) * P, P), :]
                                     ).then_inc(xs_in[j], 16)
                        sp.wait_ge(ys_ready, 2 * i + (j + 2))
                        sp.dma_start(ys_dram[bass.ds(i * (2 * P) + j * P, P), :], YS[:, j, :]
                                     ).then_inc(y_out[j], 16)
                last = SLOT_TILES - 1
                sp.wait_ge(ys_ready, SLOT_TILES + 1)
                sp.dma_start(ys_dram[last * P:(last + 1) * P, :], YS[:, last % 2, :]).then_inc(y_out[last % 2], 16)
                sp.wait_ge(y_out[1 - last % 2], 16 * (SLOT_TILES // 2))
                sp.wait_ge(y_out[last % 2], 16 * (last // 2 + 1))
                sp.sem_inc(phase_done, 1)
                sp.wait_ge(phase_done, 7)
                sp.dma_start(XR, xv).then_inc(xr_in, 16)
            sp.wait_ge(stack_in[0], 2 * NLEV * 16 * (B // 2 + 1))
            sp.wait_ge(out_done, 16 * B)

        @block.gpsimd
        def _(pool):
            pool.memset(ZERO, 0.0).then_inc(zero_made, 1)
            made = 0

            def one(ins):
                nonlocal made
                made += 1
                ins.then_inc(consts_made, 1)
                pool.wait_ge(consts_made, made)

            for ident in (IDF, IDB):
                one(pool.memset(ident[:], 0.0))
                one(pool.affine_select(out=ident[:], in_=ident[:], compare_op=ALU.not_equal, fill=1.0, base=0,
                                       pattern=[[-1, P]], channel_multiplier=1))
            one(pool.memset(SEL[:], 0.0))
            for part in range(2):
                one(pool.affine_select(out=SEL[:], in_=SEL[:], compare_op=ALU.not_equal, fill=1.0, base=-HH * part,
                                       pattern=[[-1, HH], [0, P]], channel_multiplier=1))
            one(pool.memset(ONES, 1.0))
            one(pool.affine_select(out=BEFORE, in_=ONES, compare_op=ALU.is_gt, fill=0.0, base=0,
                                   pattern=[[1, P]], channel_multiplier=-1))
            one(pool.memset(VW[:], 1.0))
            one(pool.memset(MH[:], 0.0))
            one(pool.memset(ONE8, 1.0))
            one(pool.memset(RMASK, 1.0))
            one(pool.memset(RMASK.rearrange("p (e t) -> p e t", e=E)[:, :, 0:1], 0.0))
            one(pool.iota(INTS[:, 0:E], [[-1, E]], base=E, channel_multiplier=0))
            one(pool.iota(INTS[:, E:E + NT], [[P, NT]], base=0, channel_multiplier=0))
            one(pool.iota(INTS[:, E + NT:], [[1, XS_TILES]], base=0, channel_multiplier=0))
            assert made == CONSTS

            pool.wait_ge(slots_ready, 1)
            pool.wait_ge(xs_zeroed, 64)
            for b in range(B):
                for t in range(TB * b, TB * b + TB):
                    for k in range(2):
                        pool.indirect_dma_start(xs_dram, bass.IndirectOffsetOnAxis(IDX[:, k, t:t + 1], 0),
                                                XN[:, t, :], None).then_inc(scattered[b], 16)
            for b in range(B):
                pool.wait_ge(scattered[b], 16 * 2 * TB)
                pool.sem_inc(xn_taken, 1)
            pool.sem_inc(scatter_done, 1)

            pool.wait_ge(phase_done, 7)
            for i in range(B // 2):
                for n in range(TB):
                    for t in (TB * i + n, TB * (i + B // 2) + n):
                        for k in range(2):
                            pool.indirect_dma_start(YG[:, t, k, :], None, ys_dram,
                                                    bass.IndirectOffsetOnAxis(IDX[:, k, t:t + 1], 0)
                                                    ).then_inc(gathered[i], 16)
                if i:
                    pool.wait_ge(gathered[i - 1], 16 * 4 * TB)
                    pool.sem_inc(rows_back, 1)
            pool.wait_ge(gathered[B // 2 - 1], 16 * 4 * TB)
            pool.sem_inc(rows_back, 1)
            ov = out.rearrange("(t p) d -> p t d", p=P)
            for i in range(B // 2):
                pool.wait_ge(sum_done, i + 1)
                for b in (i, i + B // 2):
                    pool.dma_start(ov[:, b * TB:(b + 1) * TB, :], XN[:, b * TB:(b + 1) * TB, :]).then_inc(out_done, 16)

        @block.scalar
        def _(act):
            c = pair_counts()
            act.dma_start(GW, gate).then_inc(consts_in, 16)
            act.dma_start(WQKV[:], wqkv).then_inc(consts_in, 16)
            act.dma_start(BQK[:], bqk).then_inc(consts_in, 16)
            act.dma_start(BV, bv).then_inc(consts_in, 16)
            act.dma_start(WOUT[:], wout).then_inc(consts_in, 16)
            act.dma_start(BOUT[:], bout).then_inc(consts_in, 16)
            act.sem_inc(probs_ready, 2)
            act.sem_inc(xt_free, 2)
            act.sem_inc(ht_free, 1)
            for g in range(4):
                act.wait_ge(var_ready, g + 1)
                act.activation(STD[:, 8 * g:8 * g + 8], VAR[:, 8 * g:8 * g + 8], ACT.Sqrt).then_inc(std_ready, 1)
            c["T"].per, c["W"].per = 1, 1
            with loop(act, NT // 2, c["T"], c["W"]) as i:
                for k, (full, free, bk, n) in enumerate(((t_full, t_free, T_BANK, c["T"]),
                                                         (w_full, w_free, W_BANK, c["W"]))):
                    act.wait_ge(full, n.add())
                    act.activation(XT[:, :, bass.ds(i * (2 * P) + k * P, P)],
                                   bk[:, 0:D].rearrange("p (c n) -> p c n", c=NC_D), ACT.Copy).then_inc(free, 1)
            c["T"].per, c["W"].per = pair_counts()["T"].per, pair_counts()["W"].per

            def take_part(blk):
                if blk == 0:
                    wait_some(act, parts_out, c["NB"].now() * (2 * NPART * 16))
                    c["NB"].add()
                act.wait_ge(w_full, c["W"].add())
                act.activation(PARTS[:, 0, blk, :], W_BANK[:, 0:SPAN], ACT.Identity,
                               bias=BQK[:, blk:blk + 1]).then_inc(part0_ready, 1)

            act.wait_ge(consts_in, 96)
            for blk in range(4):
                take_part(blk)
            act.wait_ge(gap_ready, 1)
            act.activation(E2, PA, ACT.Exp).then_inc(e2_ready, 1)
            c["W"].add(4)
            c["T"].add(1)

            def pair(stage):
                for par in range(2):
                    for u in range(UNITS):
                        if u % 2 == 1 and u > 1:
                            act.wait_ge(t_full, c["T"].add())
                            act.activation(OTS[:], T_BANK[:, 0:D].rearrange("p (c n) -> p c n", c=NC_D), ACT.Copy
                                           ).then_inc(t_free, 1)
                        for q in range(2):
                            act.wait_ge(st_full, c["ST"].add())
                            act.activation(PT[:, 2 * (u % 2) + q, :], ST_BANK[q], ACT.Exp, scale=SCALE
                                           ).then_inc(probs_ready, 1)
                        c["T"].add(1)
                        if u < 4:
                            take_part(u)
                        elif u < 7:
                            c["W"].add(1)
                    c["W"].add(1)
                    act.wait_ge(t_full, c["T"].add())
                    last = act.activation(OTS[:], T_BANK[:, 0:D].rearrange("p (c n) -> p c n", c=NC_D), ACT.Copy)
                    last.then_inc(t_free, 1)

            for stage in range(2):
                with loop(act, PAIRS, c["T"], c["W"], c["ST"], c["NB"]):
                    pair(stage)
                if stage:
                    break
                act.wait_ge(t_free, c["T"].now())
                act.sem_inc(phase_done, 1)
                act.wait_ge(phase_done, 3)

                def take_tanh(j, k):
                    act.wait_ge(h1_full, j + 1)
                    act.activation(HID[:, k, :], bank(2 * k), ACT.Tanh, scale=0.5).then_inc(tanh_ready, 1)

                def take_ht(j):
                    act.wait_ge(ht_full, j + 1)
                    act.activation(HTS, bank(6).rearrange("p (c n) -> p c n", c=FC), ACT.Copy).then_inc(ht_free, 1)

                def take_xt(j, k):
                    act.wait_ge(xt_full, j + 1)
                    act.activation(XTS[:, k], bank(4 + k)[:, 0:D].rearrange("p (c n) -> p c n", c=NC_D), ACT.Copy
                                   ).then_inc(xt_free, 1)

                take_xt(0, 0)
                take_xt(1, 1)
                take_tanh(0, 0)
                with act.Fori(0, SLOT_TILES // 2) as i:
                    for k in range(2):
                        j = 2 * i + k
                        take_tanh(j + 1, 1 - k)
                        take_ht(j)
                        take_xt(j + 2, k)
                take_ht(SLOT_TILES - 1)
                act.wait_ge(ht_free, SLOT_TILES + 1)
                act.sem_inc(phase_done, 1)
                act.wait_ge(phase_done, 7)

        @block.vector
        def _(dve):
            c = pair_counts()
            step = Count(0, 0)

            def link(ins):
                ins.then_inc(dve_step, 1)
                dve.wait_ge(dve_step, step.add())

            def tt(o, a, b, op):
                return dve.tensor_tensor(out=o, in0=a, in1=b, op=op)

            def ts(o, a, s1, s2, op0, op1):
                return dve.tensor_scalar(out=o, in0=a, scalar1=s1, scalar2=s2, op0=op0, op1=op1)

            def red(o, a, op, **kw):
                return dve.tensor_reduce(out=o, in_=a, axis=AX_X, op=op, **kw)

            def wide(v, n=E):
                return v.unsqueeze(2).to_broadcast([P, v.shape[1], n])

            for s in (o_free, r_free, ys_ready):
                dve.sem_inc(s, 1)
            dve.sem_inc(g_done, 2)
            dve.sem_inc(hid_done, 2)

            for g in range(4):
                lo, hi = 8 * g, 8 * g + 8
                dve.wait_ge(x_in[g], 16)
                step.per = 1
                with loop(dve, 8, step) as i:
                    dve.bn_stats(out=STAT[:, bass.ds(i + lo, 1), :].rearrange("p o s -> p (o s)"),
                                 in_=XN[:, bass.ds(i + lo, 1), :].rearrange("p o d -> p (o d)")).then_inc(dve_step, 1)
                    step.add()
                dve.wait_ge(dve_step, step.now())
                me, mo = STAT[:, lo:hi, 1], STAT[:, lo:hi, 4]
                ve, vo = STAT[:, lo:hi, 2], STAT[:, lo:hi, 5]
                mean, var, dif, tmp = MEAN[:, lo:hi], VAR[:, lo:hi], DIF[:, lo:hi], TMP[:, lo:hi]
                link(tt(mean, me, mo, ALU.add))
                link(ts(mean, mean, 0.5, None, ALU.mult, ALU.bypass))
                link(tt(dif, me, mo, ALU.subtract))
                link(tt(dif, dif, dif, ALU.mult))
                link(ts(dif, dif, 0.25, EPS, ALU.mult, ALU.add))
                link(tt(tmp, ve, vo, ALU.add))
                link(dve.scalar_tensor_tensor(out=var, in0=tmp, scalar=1.0 / D, in1=dif, op0=ALU.mult, op1=ALU.add))
                dve.sem_inc(var_ready, 1)
                dve.wait_ge(std_ready, g + 1)
                rs = RS[:, lo:hi]
                link(dve.reciprocal(out=rs, in_=STD[:, lo:hi]))
                link(tt(tmp, rs, rs, ALU.mult))
                link(tt(tmp, tmp, var, ALU.mult))
                link(ts(tmp, tmp, -0.5, 1.5, ALU.mult, ALU.add))
                link(tt(rs, rs, tmp, ALU.mult))
                with dve.Fori(0, 8) as i:
                    row = XN[:, bass.ds(i + lo, 1), :].rearrange("p o d -> p (o d)")
                    ts(row, row, MEAN[:, bass.ds(i + lo, 1)], RS[:, bass.ds(i + lo, 1)], ALU.subtract, ALU.mult
                       ).then_inc(xn_ready, 1)

            dve.wait_ge(consts_made, CONSTS)
            dve.tensor_copy(REV, INTS[:, 0:E])
            dve.tensor_copy(TH, INTS[:, E:E + NT])
            link(dve.tensor_copy(JI, INTS[:, E + NT:]))
            dve.wait_ge(consts_in, 96)
            for k in range(NC_D):
                dve.tensor_copy(BVB[:, k, :], BV[:, k:k + 1].to_broadcast([P, P])).then_inc(bv_ready, 1)

            def top(scores, most, one_hot):
                link(red(most, scores, ALU.max))
                link(tt(EQ, scores, wide(most), ALU.is_equal))
                link(tt(KEY, EQ, REV.unsqueeze(1).to_broadcast([P, NT, E]), ALU.mult))
                link(red(KM, KEY, ALU.max))
                link(tt(one_hot, KEY, wide(KM), ALU.is_equal))

            dve.wait_ge(gates_full, NT // 2)
            link(dve.tensor_copy(G, bank(0)[:, 0:NT * E].rearrange("p (t e) -> p t e", e=E)))
            top(G, M1, OH1)
            link(dve.scalar_tensor_tensor(out=G2, in0=OH1, scalar=FAR, in1=G, op0=ALU.mult, op1=ALU.add))
            top(G2, M2, OH2)
            tt(MASK, OH1, OH2, ALU.add).then_inc(mask_ready, 1)
            tt(PA, M2, M1, ALU.subtract).then_inc(gap_ready, 1)

            def split(blk):
                wait_some(dve, parts_ready, c["QK"].now())
                dve.wait_ge(part0_ready, c["QK"].add())
                dve.wait_ge(w_full, c["W"].add())
                dve.scalar_tensor_tensor(out=REST, in0=W_BANK[:, 0:SPAN], scalar=BQK[:, blk:blk + 1],
                                         in1=PARTS[:, 0, blk, :], op0=ALU.add, op1=ALU.subtract).then_inc(w_free, 1)
                dve.wait_ge(w_free, c["W"].now())
                link(dve.tensor_copy(PARTS[:, 1, blk, :], REST))
                tt(PARTS[:, 2, blk, :], REST, PARTS[:, 1, blk, :], ALU.subtract).then_inc(parts_ready, 1)

            def take_values(n):
                dve.wait_ge(w_full, c["W"].add())
                dve.tensor_copy(VW[:, n, :, 0:HD], W_BANK[:, 0:D].rearrange("p (h d) -> p h d", d=HD)
                                ).then_inc(w_free, 1)

            c["T"].add(NT // 2)
            c["W"].add(NT // 2)
            for blk in range(4):
                split(blk)

            dve.wait_ge(ranks_full, 1)
            ps_rank = bank(1)[:, 0:NT * E].rearrange("p (t e) -> p t e", e=E)
            ps_tot = bank(1)[:, NT * E:2 * NT * E].rearrange("p (t e) -> p e t", e=E)
            tot, inc, exc = (v.rearrange("p (e t) -> p e t", e=E) for v in (TOT, INC, EXC))
            link(dve.tensor_copy(RANK, ps_rank))
            link(dve.tensor_copy(tot, ps_tot))
            link(dve.tensor_tensor_scan(out=INC, data0=RMASK, data1=TOT, initial=0.0, op0=ALU.mult, op1=ALU.add))
            link(tt(EXC, INC, TOT, ALU.subtract))
            link(tt(CMP, inc[:, :, NT - 1:NT].to_broadcast([P, E, NT]), TH.unsqueeze(1).to_broadcast([P, E, NT]),
                    ALU.is_gt))
            link(red(NTL, CMP, ALU.add))
            link(dve.tensor_tensor_scan(out=INCT, data0=ONE8, data1=NTL, initial=0.0, op0=ALU.mult, op1=ALU.add))
            link(tt(BASE, INCT, NTL, ALU.subtract))
            link(ts(BASE, BASE, float(P), None, ALU.mult, ALU.bypass))
            link(tt(SLOT, RANK, exc.rearrange("p e t -> p t e"), ALU.add))
            link(tt(SLOT, SLOT, BASE.unsqueeze(1).to_broadcast([P, NT, E]), ALU.add))
            for k, one_hot in enumerate((OH1, OH2)):
                link(tt(PICK, SLOT, one_hot, ALU.mult))
                link(red(SLOTF[:, k, :], PICK, ALU.add))
            dve.tensor_copy(IDX[:], SLOTF).then_inc(slots_ready, 1)
            link(tt(CMPJ, INCT.unsqueeze(1).to_broadcast([P, XS_TILES, E]), wide(JI), ALU.is_le))
            link(red(EJF, CMPJ, ALU.add))
            link(ts(EJF, EJF, float(E - 1), None, ALU.min, ALU.bypass))
            link(dve.tensor_copy(EJ[:], EJF[0:1, :]))
            dve.wait_ge(e2_ready, 1)
            link(ts(M1, E2, 1.0, None, ALU.add, ALU.bypass))
            link(dve.reciprocal(out=M2, in_=M1))
            ts(PW[:, 0, :], M2, 0.5, None, ALU.mult, ALU.bypass)
            link(dve.scalar_tensor_tensor(out=PW[:, 1, :], in0=E2, scalar=0.5, in1=M2, op0=ALU.mult, op1=ALU.mult))
            dve.wait_ge(r_full, 1)
            tt(BOUT[:], BOUT[:], R_BANK[:, 0:D], ALU.add).then_inc(r_free, 1)
            c["R"].add(1)
            for n in range(NWIN):
                take_values(n)

            def take_max():
                wait_some(dve, mh_ready, c["S"].now())
                dve.wait_ge(s_full, c["S"].add())
                red(MNEG[:], S_BANKS.rearrange("p (h k) -> p h k", k=WIN), ALU.max, negate=True).then_inc(s_free, 1)
                dve.wait_ge(s_free, c["S"].now())
                link(dve.tensor_copy(MH[:, 0:HH], MNEG[:]))
                tt(MH[:, HH:2 * HH], MNEG[:], MH[:, 0:HH], ALU.subtract).then_inc(mh_ready, 1)

            def take_negm(k):
                dve.wait_ge(t_full, c["T"].add())
                dve.tensor_copy(NEGM[:, k, :], T_BANK[0:STK, 0:P // 2].bitcast(BF16)).then_inc(t_free, 1)

            take_max()
            take_negm(0)

            def norm():
                dve.wait_ge(o_free, c["O"].now() + 1)
                dve.wait_ge(o_full, c["O"].add())
                o = O_BANK[:, 0:H * (HD + 1)].rearrange("p (h d) -> p h d", d=HD + 1)
                link(dve.reciprocal(out=RDEN[:], in_=o[:, :, HD]))
                tt(OSB[:], o[:, :, 0:HD], RDEN[:].unsqueeze(2).to_broadcast([P, H, HD]), ALU.mult
                   ).then_inc(o_free, 1)

            def row(t):
                return XN[:, bass.ds(t, 1), :].rearrange("p o d -> p (o d)")

            def combine(t, last):
                y = YG[:, bass.ds(t, 1), :, :]
                for k in range(2):
                    link(dve.scalar_tensor_tensor(out=row(t), in0=y[:, :, k, :].rearrange("p o d -> p (o d)"),
                                                  scalar=PW[:, k, bass.ds(t, 1)], in1=row(t),
                                                  op0=ALU.mult, op1=ALU.add))
                ins = tt(row(t), row(t), XR[:, bass.ds(t, 1), :].rearrange("p o d -> p (o d)"), ALU.add)
                if last:
                    ins.then_inc(sum_done, 1)

            def project(stage, b, n):
                dve.wait_ge(r_full, c["R"].add())
                ins = tt(row(b * TB + n), R_BANK[:, 0:D], BOUT[:], ALU.add)
                ins.then_inc(r_free, 1)
                if stage:
                    dve.wait_ge(r_free, c["R"].now() + 1)
                    combine(b * TB + n, False)
                    combine(b * TB + n - NT // 2, n == NWIN - 1)

            for stage in range(2):
                if stage:
                    dve.wait_ge(xr_in, 16)
                step.per = PAIR_STEPS[stage]
                with loop(dve, PAIRS, step, c["T"], c["W"], c["S"], c["O"], c["R"], c["QK"]) as i:
                    for par in range(2):
                        b = 4 * stage + 2 * i + par
                        dve.wait_ge(xn_taken, b + 1)
                        if stage:
                            dve.wait_ge(rows_back, 2 * i + par + 1)
                        for u in range(UNITS):
                            if u % 2 == 1 and u > 1:
                                c["T"].add(1)
                            take_max()
                            take_negm((u + 1) % 2)
                            if u % 2 == 1 and u > 1:
                                project(stage, b, u // 2 - 1)
                            if u % 2 == 0 and u > 1:
                                norm()
                            if u < 4:
                                split(u)
                            elif u < 7:
                                take_values(u - 4)
                        norm()
                        take_values(3)
                        c["T"].add(1)
                        project(stage, b, NWIN - 1)
                if stage:
                    break
                dve.wait_ge(r_free, c["R"].now() + 1)
                dve.sem_inc(phase_done, 1)
                dve.wait_ge(phase_done, 3)

                def hidden(j, k):
                    dve.wait_ge(tanh_ready, j + 1)
                    dve.scalar_tensor_tensor(out=HID[:, k, :], in0=HID[:, k, :], scalar=1.0, in1=bank(2 * k),
                                             op0=ALU.add, op1=ALU.mult).then_inc(g_done, 1)
                    dve.wait_ge(g_done, j + 3)
                    dve.wait_ge(h2_full, j + 1)
                    tt(HID[:, k, :], HID[:, k, :], bank(2 * k + 1), ALU.mult).then_inc(hid_done, 1)

                def take_y(j, k, stored):
                    dve.wait_ge(y_full, j + 1)
                    wait_some(dve, y_out[k], 16 * stored)
                    dve.tensor_copy(YS[:, k, :], bank(7)[:, 0:D]).then_inc(ys_ready, 1)

                hidden(0, 0)
                for k in range(2):
                    hidden(k + 1, 1 - k)
                    take_y(k, k, 0)
                with dve.Fori(1, SLOT_TILES // 2) as i:
                    for k in range(2):
                        hidden(2 * i + k + 1, 1 - k)
                        take_y(2 * i + k, k, i)
                take_y(SLOT_TILES - 1, (SLOT_TILES - 1) % 2, SLOT_TILES // 2)
                dve.wait_ge(ys_ready, SLOT_TILES)
                dve.sem_inc(phase_done, 1)
                dve.wait_ge(phase_done, 7)

        @block.tensor
        def _(pe):
            c = pair_counts()

            def mm(o, a, b, start=True, stop=True):
                return pe.matmul(o, a, b, start=start, stop=stop)

            pe.wait_ge(consts_made, CONSTS)
            pe.wait_ge(consts_in, 96)
            for i in range(NT // 2):
                for k, (full, free, bk) in enumerate(((t_full, t_free, T_BANK), (w_full, w_free, W_BANK))):
                    pe.wait_ge(xn_ready, 2 * i + k + 1)
                    if i:
                        pe.wait_ge(free, i)
                    for ch in range(NC_D):
                        last = pe.transpose(bk[:, ch * P:(ch + 1) * P], XN[:, 2 * i + k, ch * P:(ch + 1) * P], IDF[:])
                    last.then_inc(full, 1)
                for k, free in enumerate((t_free, w_free)):
                    t = 2 * i + k
                    pe.wait_ge(free, i + 1)
                    for ch in range(NC_D):
                        last = mm(bank(0)[:, t * E:(t + 1) * E], XT[:, ch, t * P:(t + 1) * P], GW[:, ch, :],
                                  ch == 0, ch == NC_D - 1)
                last.then_inc(gates_full, 1)
            c["T"].add(NT // 2)
            c["W"].add(NT // 2)

            def queries_keys(blk, xt):
                pe.wait_ge(w_free, c["W"].now())
                for ch in range(NC_D):
                    last = mm(W_BANK[:, 0:SPAN], WQKV[:, ch, blk * P:(blk + 1) * P], xt[:, ch, 0:SPAN],
                              ch == 0, ch == NC_D - 1)
                last.then_inc(w_full, 1)
                c["W"].add()

            def values(n, xt):
                pe.wait_ge(w_free, c["W"].now())
                for ch in range(NC_D):
                    last = mm(W_BANK[:, 0:D], xt[:, ch, n * STRIDE:n * STRIDE + WIN], WQKV[:, ch, 2 * D:3 * D],
                              ch == 0, ch == NC_D - 1)
                last.then_inc(w_full, 1)
                c["W"].add()

            for blk in range(4):
                queries_keys(blk, XT)
            pe.wait_ge(mask_ready, 1)
            mm(bank(1)[:, 0:NT * E], BEFORE, MASK.rearrange("p t e -> p (t e)"))
            mm(bank(1)[:, NT * E:2 * NT * E], ONES, MASK.rearrange("p t e -> p (t e)")).then_inc(ranks_full, 1)
            pe.wait_ge(bv_ready, NC_D)
            for ch in range(NC_D):
                last = mm(R_BANK[:, 0:D], BVB[:, ch, :], WOUT[:, ch, :], ch == 0, ch == NC_D - 1)
            last.then_inc(r_full, 1)
            c["R"].add(1)
            for n in range(NWIN):
                values(n, XT)

            def scores(par, u):
                n, half = u // 2, u % 2
                wait_some(pe, s_free, c["S"].now())
                w = slice(n * STRIDE, n * STRIDE + WIN)
                for h in range(HH):
                    last = mm(S_BANKS[:, h * WIN:(h + 1) * WIN], QS[:, par, half * HH + h, w],
                              KS[:, par, half * HH + h, w])
                last.then_inc(s_full, 1)
                c["S"].add()

            def shift_row():
                pe.wait_ge(mh_ready, c["S"].now())
                pe.wait_ge(t_free, c["T"].now())
                pe.transpose(T_BANK[0:STK, 0:P // 2].bitcast(BF16), MH[:], IDB[:]).then_inc(t_full, 1)
                c["T"].add()

            def shifted(par, u):
                n, half = u // 2, u % 2
                w = slice(n * STRIDE, n * STRIDE + WIN)
                for q in range(2):
                    pe.wait_ge(probs_ready, c["ST"].now() + 1)
                    for hq in range(HQ):
                        h = q * HQ + hq
                        o = ST_BANK[q][:, hq * WIN:(hq + 1) * WIN]
                        mm(o, KS[:, par, half * HH + h, w], QS[:, par, half * HH + h, w], True, False)
                        last = mm(o, SEL[:, h, :], NEGM[:, u % 2, :], False, True)
                    last.then_inc(st_full, 1)
                    c["ST"].add()

            def weighted(u, behind):
                n, half = u // 2, u % 2
                if half == 0:
                    pe.wait_ge(o_free, c["O"].now() + 1)
                pe.wait_ge(probs_ready, c["ST"].now() + 2 - behind)
                for h in range(HH):
                    hh = half * HH + h
                    last = mm(O_BANK[:, hh * (HD + 1):(hh + 1) * (HD + 1)],
                              PT[:, 2 * (u % 2) + h // HQ, (h % HQ) * WIN:(h % HQ + 1) * WIN], VW[:, n, hh, :])
                if half:
                    last.then_inc(o_full, 1)
                    c["O"].add()

            def turn():
                pe.wait_ge(o_free, c["O"].now() + 1)
                pe.wait_ge(t_free, c["T"].now())
                for ch in range(NC_D):
                    last = pe.transpose(T_BANK[:, ch * P:(ch + 1) * P],
                                        OSB[:].rearrange("p h d -> p (h d)")[:, ch * P:(ch + 1) * P], IDF[:])
                last.then_inc(t_full, 1)
                c["T"].add()

            def project(tfree):
                pe.wait_ge(t_free, tfree)
                pe.wait_ge(r_free, c["R"].now() + 1)
                for ch in range(NC_D):
                    last = mm(R_BANK[:, 0:D], OTS[:, ch, :], WOUT[:, ch, :], ch == 0, ch == NC_D - 1)
                last.then_inc(r_full, 1)
                c["R"].add()

            pe.wait_ge(stack_in[0], 2 * NLEV * 16)
            pe.wait_ge(slots_ready, 1)
            scores(0, 0)
            shift_row()
            loads = Count(2 * NLEV * 16, 2 * NLEV * 16)

            for stage in range(2):
                with loop(pe, PAIRS, c["T"], c["W"], c["S"], c["ST"], c["O"], c["R"], loads) as i:
                    for par in range(2):
                        b = 2 * i + (4 * stage + par)
                        for u in range(UNITS):
                            if u < UNITS - 1:
                                scores(par, u + 1)
                            else:
                                if par == 1:
                                    loads.add(2 * NLEV * 16)
                                pe.wait_ge(stack_in[1 - par], loads.now())
                                scores(1 - par, 0)
                            if u % 2 == 1 and u > 1:
                                turn()
                            pe.wait_ge(t_free, c["T"].now(1 if u % 2 == 1 and u > 1 else 0))
                            shifted(par, u)
                            if u > 0:
                                weighted(u - 1, 2)
                            if u % 2 == 1 and u > 1:
                                project(c["T"].now())
                            shift_row()
                            if u == 0:
                                pe.wait_ge(xnt_in, b * 16 + 16)
                            if u < 4:
                                queries_keys(u, XNT)
                            elif u < 7:
                                values(u - 4, XNT)
                        weighted(UNITS - 1, 0)
                        values(3, XNT)
                        turn()
                        project(c["T"].now())
                if stage:
                    break
                pe.wait_ge(r_full, c["R"].now())
                pe.sem_inc(phase_done, 1)
                pe.wait_ge(phase_done, 3)
                pe.wait_ge(weights_in, 16 * E)

                def tokens(j, k):
                    pe.wait_ge(xs_in[k], (j - k) * 8 + 16)
                    pe.wait_ge(xt_free, j + 1)
                    for ch in range(NC_D):
                        last = pe.transpose(bank(4 + k)[:, ch * P:(ch + 1) * P], XS[:, k, ch * P:(ch + 1) * P], IDF[:])
                    last.then_inc(xt_full, 1)

                def up(j, k, half, at):
                    full, free = ((h1_full, g_done), (h2_full, hid_done))[half]
                    if half == 0:
                        pe.wait_ge(xt_free, j + 3)
                    pe.wait_ge(free, j + 1)
                    for ch in range(NC_D):
                        last = mm(bank(2 * k + half), XTS[:, k, ch, :],
                                  WALL[:, bass.ds(at + (ch * 2 + half) * FH, FH)], ch == 0, ch == NC_D - 1)
                    last.then_inc(full, 1)

                def turn_hidden(j, k):
                    pe.wait_ge(hid_done, j + 3)
                    pe.wait_ge(ht_free, j + 1)
                    for f in range(FC):
                        last = pe.transpose(bank(6)[:, f * P:(f + 1) * P], HID[:, k, f * P:(f + 1) * P], IDF[:])
                    last.then_inc(ht_full, 1)

                def down(j, at):
                    pe.wait_ge(ht_free, j + 2)
                    pe.wait_ge(ys_ready, j + 1)
                    for f in range(FC):
                        last = mm(bank(7)[:, 0:D], HTS[:, f, :],
                                  WALL[:, bass.ds(at + 2 * NC_D * FH + f * D, D)], f == 0, f == FC - 1)
                    last.then_inc(y_full, 1)

                def expert(j):
                    return pe.value_load(EJ[0:1, bass.ds(j, 1)], min_val=0, max_val=E - 1) * WE

                tokens(0, 0)
                tokens(1, 1)
                at0 = expert(0)
                up(0, 0, 0, at0)
                up(0, 0, 1, at0)
                with pe.Fori(0, SLOT_TILES // 2) as i:
                    for k in range(2):
                        j = 2 * i + k
                        nxt = expert(j + 1)
                        up(j + 1, 1 - k, 0, nxt)
                        if k == 0:
                            this = expert(j)
                        turn_hidden(j, k)
                        up(j + 1, 1 - k, 1, nxt)
                        tokens(j + 2, k)
                        down(j, this)
                        this = nxt
                j = SLOT_TILES - 1
                turn_hidden(j, j % 2)
                down(j, expert(j))
                pe.wait_ge(y_full, SLOT_TILES)
                pe.sem_inc(phase_done, 1)
                pe.wait_ge(phase_done, 7)


_NAMES = ("L0_attn_x", "L0_attn_w_qkv", "L0_attn_b_qkv", "L0_attn_w_out", "L0_attn_b_out", "L0_ffn_w12", "L0_ffn_w3",
          "L0_ffn_gate_w")


def kernel(**inputs):
    import numpy as np
    import concourse.bacc as bacc
    from concourse.bass_utils import run_bass_kernel_spmd

    x, w_qkv, b_qkv, w_out, b_out, w12, w3, gate_w = (np.asarray(inputs[n]) for n in _NAMES)

    def down(w):
        return w.reshape(-1, P, w.shape[-1]).transpose(1, 0, 2).reshape(P, -1)

    w12_t = w12.transpose(0, 2, 1).reshape(E, NC_D, P, 2 * FH).transpose(2, 0, 1, 3).reshape(P, E, -1)
    w3_t = w3.transpose(0, 2, 1).reshape(E, FC, P, D).transpose(2, 0, 1, 3).reshape(P, E, -1)
    arrays = {
        "x": x.reshape(B * L, D),
        "wqkv": down(w_qkv),
        "bqk": b_qkv[:2 * D].reshape(4, P).T,
        "bv": b_qkv[2 * D:].reshape(NC_D, P).T,
        "wout": down(w_out),
        "bout": np.broadcast_to(b_out, (P, D)),
        "gate": down(gate_w.T),
        "wexp": np.concatenate([w12_t, w3_t], axis=2).reshape(P, E * WE),
    }
    arrays = {f"in_{k}": np.ascontiguousarray(v) for k, v in arrays.items()}
    nc = bacc.Bacc("TRN2", target_bir_lowering=False, num_devices=1)
    args = [nc.dram_tensor(k, v.shape, mybir.dt.from_np(v.dtype), kind="ExternalInput").ap()
            for k, v in arrays.items()]
    args.append(nc.dram_tensor("out_0", (B * L, D), F32, kind="ExternalOutput").ap())
    layer(nc, *args)
    r = run_bass_kernel_spmd(nc, [arrays], core_ids=[0])
    return r.results[0]["out_0"].reshape(B, L, D)
```

```python
from contextlib import ExitStack, contextmanager

import concourse.bass as bass
from concourse import mybir

F32 = mybir.dt.float32
BF16 = mybir.dt.bfloat16
F32R = mybir.dt.float32r
I32 = mybir.dt.int32
U32 = mybir.dt.uint32
ALU = mybir.AluOpType
ACT = mybir.ActivationFunctionType
AX_X = mybir.AxisListType.X

P = 128
B, L, D = 8, 512, 256
NC_D = D // P
TB = L // P
NT = B * TB
H, HD = 16, 16
WIN, STRIDE = 128, 64
NWIN = L // WIN
SPAN = STRIDE * (NWIN - 1) + WIN
HH = H // 2
UNITS = 2 * NWIN
HQ = HH // 2
SCALE = float(HD) ** -0.5
E, FH = 8, 512
FC = FH // P
SLOT_TILES = (2 * B * L + E * (P - 1)) // P
XS_TILES = SLOT_TILES + 1
XS_LOADS = XS_TILES + 1
WE = NC_D * 2 * FH + FC * D
EPS = 1e-5
BANK = 512
FAR = -3.0e38
Q_LEVELS = (0, 0, 1, 0, 2, 1)
K_LEVELS = (0, 1, 0, 2, 0, 1)
NLEV = len(Q_LEVELS)
STK = NLEV * HD
NPART = 3
PARTS_OUT = 4 * NPART * 16
PAIRS = 2


class Count:

    def __init__(self, start=0, per=0):
        self.base, self.n, self.per = start, 0, per

    def add(self, k=1):
        self.n += k
        return self.base + self.n

    def now(self, less=0):
        return self.base + (self.n - less)


@contextmanager
def loop(eng, times, *counts):
    starts = [c.now() for c in counts]
    with eng.Fori(0, times) as i:
        for c, s in zip(counts, starts):
            c.base, c.n = i * c.per + s, 0
        yield i
        for c in counts:
            assert c.n == c.per, (c.n, c.per)
    for c, s in zip(counts, starts):
        c.base, c.n = s + times * c.per, 0


def wait_some(eng, sem, value):
    if not (isinstance(value, int) and value == 0):
        eng.wait_ge(sem, value)


def layer(nc, x, wqkv, bqk, bv, wout, bout, gate, wexp, out):
    with ExitStack() as ctx:
        def sb(name, shape, dt=F32):
            return ctx.enter_context(nc.sbuf_tensor(name, shape, dt))

        def shared(name, shape, dt):
            with nc.sbuf_tensor(name, shape, dt) as buffer:
                return buffer

        def sem(name):
            return ctx.enter_context(nc.semaphore(name))

        xs_dram = nc.dram_tensor("xs_scratch", (XS_LOADS * P, D), F32, kind="Internal").ap()
        ys_dram = nc.dram_tensor("ys_scratch", (SLOT_TILES * P, D), F32, kind="Internal").ap()
        pd_dram = nc.dram_tensor("parts_scratch", (B + 1, NPART, 2, H, HD, SPAN), BF16, kind="Internal").ap()
        xt_dram = nc.dram_tensor("xt_scratch", (B + 2, P, NC_D, SPAN), F32, kind="Internal").ap()

        rows_dram = nc.dram_tensor("rows_scratch", (B // 2 * L, D), F32, kind="Internal").ap()

        WS = shared("WS", [P, 2, 2, 2, NC_D, FH], F32R)
        XN = sb("XN", [P, NT, D])
        WALL = sb("WALL", [P, E * WE])
        QS = sb("QS", [STK, 2, H, SPAN], BF16)
        KS = sb("KS", [STK, 2, H, SPAN], BF16)
        XTS = shared("XTS", [P, 2, 2, NC_D, P], F32R)
        WORK = sb("WORK", [P, 4928])
        VW = sb("VW", [P, NWIN, H, HD + 1])
        WQKV = sb("WQKV", [P, NC_D, 3 * D])
        WOUT = sb("WOUT", [P, NC_D, D])
        BOUT = sb("BOUT", [P, D])
        BQK = sb("BQK", [P, 4])
        IDF = sb("IDF", [P, P])
        IDB = sb("IDB", [P, P], BF16)
        SEL = sb("SEL", [STK, HH, P], BF16)
        OSB = sb("OSB", [P, H, HD])
        OTS = sb("OTS", [P, NC_D, P])
        MNEG = sb("MNEG", [P, HH])
        MH = sb("MH", [P, STK], BF16)
        NEGM = sb("NEGM", [STK, 2, P], BF16)
        RDEN = sb("RDEN", [P, H])
        PW = sb("PW", [P, 2, NT])
        IDX = sb("IDX", [P, 2, NT], U32)
        EJ = sb("EJ", [1, XS_TILES], I32)

        nq = 4 * SPAN // 2
        PARTS = WORK[:, 0:NPART * nq].bitcast(BF16).rearrange("p (l k t) -> p l k t", l=NPART, k=4)
        at = NPART * nq
        REST = WORK[:, at:at + SPAN]
        at += SPAN
        XNT = WORK[:, at:at + NC_D * SPAN].rearrange("p (c t) -> p c t", c=NC_D)
        at += NC_D * SPAN
        PT = WORK[:, at:at + 4 * BANK].rearrange("p (r n) -> p r n", r=4)
        assert at + 4 * BANK <= 4928
        at = 0

        def work(n):
            nonlocal at
            at += n
            assert at <= 4928
            return WORK[:, at - n:at]

        work(4 * D)
        XS = work(2 * D).rearrange("p (b n) -> p b n", b=2)
        HTS = work(FH).rearrange("p (c n) -> p c n", c=FC)
        assert at <= NPART * nq + SPAN
        at = NPART * nq + 3 * SPAN + 2 * BANK
        HID = work(2 * FH).rearrange("p (b n) -> p b n", b=2)
        YS = (OSB[:].rearrange("p h d -> p (h d)"), OTS[:].rearrange("p c n -> p (c n)"))
        at = 0

        def temp(n, dt=F32):
            nonlocal at
            at += n
            assert at <= E * WE
            v = WALL[:, at - n:at]
            return v if dt == F32 else v.bitcast(dt)

        ZERO = temp(XS_LOADS * D // 4)
        XT = temp(NC_D * NT * P).rearrange("p (c n) -> p c n", c=NC_D)
        GW = temp(NC_D * E).rearrange("p (c e) -> p c e", c=NC_D)
        BV = temp(NC_D)
        BVB = temp(NC_D * P).rearrange("p (c n) -> p c n", c=NC_D)
        BEFORE = temp(P)
        ONES = temp(P)
        STAT = temp(NT * 6).rearrange("p (t s) -> p t s", s=6)
        MEAN, VAR, DIF, STD, RS, TMP = (temp(NT) for _ in range(6))
        G, EQ, KEY, OH1, G2, OH2, MASK, RANK, SLOT, PICK = (
            temp(NT * E).rearrange("p (t e) -> p t e", e=E) for _ in range(10))
        TOT, INC, EXC, RMASK = (temp(NT * E) for _ in range(4))
        M1, KM, M2, E2, PA = (temp(NT) for _ in range(5))
        REV, NTL, INCT, BASE = (temp(E) for _ in range(4))
        ONE8 = temp(E)
        TH = temp(NT)
        CMP = temp(E * NT).rearrange("p (e t) -> p e t", e=E)
        JI = temp(XS_TILES)
        CMPJ = temp(XS_TILES * E).rearrange("p (j e) -> p j e", e=E)
        EJF = temp(XS_TILES)
        INTS = temp(E + NT + XS_TILES, I32)
        SLOTF = temp(2 * NT).rearrange("p (k t) -> p k t", k=2)
        assert 2 * NT * D + NT * D == E * WE
        YG = WALL[:, 0:2 * NT * D].rearrange("p (t k d) -> p t k d", k=2, d=D)
        XR = WALL[:, 2 * NT * D:].rearrange("p (t d) -> p t d", d=D)

        PS = ctx.enter_context(nc.psum_tensor("PS", [P, 8 * BANK], F32))

        def bank(k, n=1):
            return PS[:, k * BANK:(k + n) * BANK]

        S_BANKS = bank(0, 2)
        ST_BANK = (bank(2), bank(3))
        O_BANK, T_BANK, W_BANK, R_BANK = bank(4), bank(5), bank(6), bank(7)
        TOK_BANK = (bank(5), bank(6))
        FIRST_BANK = (bank(2), bank(3), bank(4), bank(7))
        FIRST_STEPS = (5, 7, 9, 11)
        BV_BANK = bank(0)[:, NT * E:NT * E + D]

        x_in = [sem(f"x_in{g}") for g in range(4)]
        gate_in = sem("gate_in")
        consts_in = sem("consts_in")
        consts_made = sem("consts_made")
        zero_made = sem("zero_made")
        xs_zeroed = sem("xs_zeroed")
        var_ready = sem("var_ready")
        std_ready = sem("std_ready")
        xn_ready = sem("xn_ready")
        tok_full, tok_free = sem("tok_full"), sem("tok_free")
        gates_full = sem("gates_full")
        first_full = sem("first_full")
        values_taken = sem("values_taken")
        temps_done = sem("temps_done")
        xt_out = sem("xt_out")
        xnt_in = sem("xnt_in")
        bv_ready, bv_full = sem("bv_ready"), sem("bv_full")
        mask_ready = sem("mask_ready")
        ranks_full, ranks_taken = sem("ranks_full"), sem("ranks_taken")
        gap_ready = sem("gap_ready")
        e2_ready = sem("e2_ready")
        slots_ready = sem("slots_ready")
        scattered = [sem(f"scattered{b}") for b in range(B)]
        xn_taken = sem("xn_taken")
        t_full, t_free = sem("t_full"), sem("t_free")
        w_full, w_free = sem("w_full"), sem("w_free")
        s_full, s_free = sem("s_full"), sem("s_free")
        mh_ready = sem("mh_ready")
        st_full, probs_ready = sem("st_full"), sem("probs_ready")
        o_full, o_free = sem("o_full"), sem("o_free")
        r_full, r_free = sem("r_full"), sem("r_free")
        part0_ready = sem("part0_ready")
        parts_ready = sem("parts_ready")
        parts_out = sem("parts_out")
        stack_in = [sem("stack_in0"), sem("stack_in1")]
        weights_in = sem("weights_in")
        phase_done = sem("phase_done")
        y_stored = sem("y_stored")
        xs_in = [sem("xs_in0"), sem("xs_in1")]
        xt_full, xt_high, xt_free = sem("xt_full"), sem("xt_high"), sem("xt_free")
        rows_out = sem("rows_out")
        high_ready = [sem("high_ready0"), sem("high_ready1")]
        low_ready = [sem("low_ready0"), sem("low_ready1")]
        h1_full, tanh_ready, g_done = sem("h1_full"), sem("tanh_ready"), sem("g_done")
        h2_full, hid_done = sem("h2_full"), sem("hid_done")
        ht_full, ht_free = sem("ht_full"), sem("ht_free")
        y_full, ys_ready = sem("y_full"), sem("ys_ready")
        y_out = [sem("y_out0"), sem("y_out1")]
        gathered = [sem(f"gathered{b}") for b in range(B)]
        xr_in = [sem(f"xr_in{b}") for b in range(B)]
        rest_ready = sem("rest_ready")
        pool_step = sem("pool_step")
        out_done = sem("out_done")
        dve_step = sem("dve_step")

        block = ctx.enter_context(nc.Block())

        def pair_counts():
            return dict(T=Count(0, 2 * (UNITS + NWIN)), W=Count(0, 2 * 8), S=Count(0, 2 * UNITS),
                        ST=Count(0, 4 * UNITS), O=Count(0, 2 * NWIN), R=Count(0, 2 * NWIN),
                        NB=Count(0, 2), QK=Count(0, 8))

        CONSTS = 17
        PAIR_STEPS = 2 * (UNITS + NWIN + 4)
        LAST_ORDER = [b for i in range(B // 2) for b in (i + B // 2, i)]

        def weights_of(eng, j, half):
            at = eng.value_load(EJ[0:1, bass.ds(j, 1)], min_val=0, max_val=E - 1) * WE
            return WALL[:, bass.ds(at, 2 * NC_D * FH)].rearrange("p (c h n) -> p c h n", c=NC_D, h=2)[:, :, half, :]

        def low_part(eng, j, k, half):
            weights = weights_of(eng, j, half)
            eng.wait_ge(high_ready[half], j + 1)
            eng.tensor_tensor(out=WS[:, k, half, 1], in0=weights, in1=WS[:, k, half, 0].bitcast(F32),
                              op=ALU.subtract).then_inc(low_ready[half], 1)

        @block.sync
        def _(sp):
            xv = x.rearrange("(t p) d -> p t d", p=P)
            for g in range(4):
                sp.dma_start(XN[:, 8 * g:8 * g + 8, :], xv[:, 8 * g:8 * g + 8, :]).then_inc(x_in[g], 16)
            sp.wait_ge(zero_made, 1)
            zv = xs_dram.rearrange("(p r) d -> p (r d)", p=P)
            q = XS_LOADS * D // 4
            for g in range(4):
                sp.dma_start(zv[:, g * q:(g + 1) * q], ZERO).then_inc(xs_zeroed, 16)

            def stacks(nb, par, weights=None):
                def of(l, k):
                    return pd_dram[bass.ds(nb, 1), l, k].rearrange("o h d t -> (o h d) t")

                for k, (stack, lev) in enumerate(((QS, Q_LEVELS), (KS, K_LEVELS))):
                    for blk in (2 * k, 2 * k + 1):
                        sp.wait_ge(parts_ready, nb * 4 + (blk + 1))
                        for l in range(NPART):
                            sp.dma_start(of(l, k)[(blk % 2) * P:(blk % 2 + 1) * P], PARTS[:, l, blk, :]
                                         ).then_inc(parts_out, 16)
                    sp.wait_ge(parts_out, nb * PARTS_OUT + (k + 1) * (PARTS_OUT // 2))
                    for l in range(NLEV):
                        sp.dma_start(stack[HD * l:HD * l + HD, par], of(lev[l], k).rearrange("(h d) t -> d h t", d=HD)
                                     ).then_inc(stack_in[par], 16)
                    if weights and k == 0:
                        weights(1)

            stacks(0, 0)

            def load_tokens(b, first=False):
                if not first:
                    sp.wait_ge(w_full, b * 8)
                sp.dma_start(XNT, xt_dram[bass.ds(b + 1, 1)].rearrange("o p c t -> (o p) c t")).then_inc(xnt_in, 16)

            sp.wait_ge(xt_out, 16 * (B + 1))
            load_tokens(0, True)
            sp.wait_ge(temps_done, 1)
            sp.wait_ge(first_full, 4 + NWIN)
            sp.wait_ge(xs_zeroed, 64)
            for stage in range(2):
                with sp.Fori(0, PAIRS) as i:
                    for par in range(2):
                        b = 2 * i + (4 * stage + par)
                        sp.wait_ge(r_free, b * NWIN + 1)
                        def weights(k):
                            w = bass.ds(b * (2 * WE) + k * WE, WE)
                            sp.dma_start(WALL[:, w], wexp[:, w]).then_inc(weights_in, 16)

                        if stage == 0:
                            weights(0)
                        stacks(b + 1, 1 - par, None if stage else weights)
                        load_tokens(b + 1)
                        if stage == 0:
                            sp.wait_ge(r_free, b * NWIN + (NWIN + 1))
                            sp.dma_start(rows_dram[bass.ds(b * L, L), :].rearrange("(t p) d -> p t d", p=P),
                                         XN[:, bass.ds(b * TB, TB), :]).then_inc(rows_out, 16)
                if stage:
                    break
                sp.wait_ge(xn_taken, B)
                sp.wait_ge(phase_done, 3)
                for j in range(3):
                    if j == 2:
                        sp.wait_ge(xt_full, 1)
                    sp.dma_start(XS[:, j % 2, :], xs_dram[j * P:(j + 1) * P, :]).then_inc(xs_in[j % 2], 16)
                with sp.Fori(0, SLOT_TILES // 2) as i:
                    for j in range(2):
                        sp.wait_ge(xt_full, 2 * i + (j + 2))
                        sp.dma_start(XS[:, 1 - j, :], xs_dram[bass.ds(i * (2 * P) + (j + 3) * P, P), :]
                                     ).then_inc(xs_in[1 - j], 16)
                        sp.wait_ge(ys_ready, 2 * i + (j + 2))
                        sp.dma_start(ys_dram[bass.ds(i * (2 * P) + j * P, P), :], YS[j]).then_inc(y_out[j], 16)
                sp.wait_ge(xs_in[0], 16 * (XS_LOADS + 1) // 2)
                sp.sem_inc(phase_done, 1)
                last = SLOT_TILES - 1
                sp.wait_ge(ys_ready, SLOT_TILES + 1)
                sp.dma_start(ys_dram[last * P:(last + 1) * P, :], YS[last % 2]).then_inc(y_out[last % 2], 16)
                sp.wait_ge(y_out[1 - last % 2], 16 * (SLOT_TILES // 2))
                sp.wait_ge(y_out[last % 2], 16 * (last // 2 + 1))
                sp.sem_inc(y_stored, 1)
                sp.wait_ge(phase_done, 8)
                rv = rows_dram.rearrange("(t p) d -> p t d", p=P)
                for b in LAST_ORDER:
                    if b < B // 2:
                        sp.dma_start(XN[:, b * TB:(b + 1) * TB, :], rv[:, b * TB:(b + 1) * TB, :]).then_inc(xr_in[b], 16)
                    sp.dma_start(XR[:, b * TB:(b + 1) * TB, :], xv[:, b * TB:(b + 1) * TB, :]).then_inc(xr_in[b], 16)
            sp.wait_ge(stack_in[0], 2 * NLEV * 16 * (B // 2 + 1))
            sp.wait_ge(xnt_in, 16 * (B + 1))
            sp.wait_ge(out_done, 16 * (B - 1 + TB))

        @block.gpsimd
        def _(pool):
            made = 0

            def one(ins):
                nonlocal made
                made += 1
                ins.then_inc(consts_made, 1)
                pool.wait_ge(consts_made, made)

            for ident in (IDF, IDB):
                one(pool.memset(ident[:], 0.0))
                one(pool.affine_select(out=ident[:], in_=ident[:], compare_op=ALU.not_equal, fill=1.0, base=0,
                                       pattern=[[-1, P]], channel_multiplier=1))
                if ident is IDF:
                    pool.memset(ZERO, 0.0).then_inc(zero_made, 1)
            one(pool.memset(SEL[:], 0.0))
            for part in range(2):
                one(pool.affine_select(out=SEL[:], in_=SEL[:], compare_op=ALU.not_equal, fill=1.0, base=-HH * part,
                                       pattern=[[-1, HH], [0, P]], channel_multiplier=1))
            one(pool.memset(ONES, 1.0))
            one(pool.affine_select(out=BEFORE, in_=ONES, compare_op=ALU.is_gt, fill=0.0, base=0,
                                   pattern=[[1, P]], channel_multiplier=-1))
            one(pool.memset(VW[:], 1.0))
            one(pool.memset(MH[:], 0.0))
            one(pool.memset(ONE8, 1.0))
            one(pool.memset(RMASK, 1.0))
            one(pool.memset(RMASK.rearrange("p (e t) -> p e t", e=E)[:, :, 0:1], 0.0))
            one(pool.iota(INTS[:, 0:E], [[-1, E]], base=E, channel_multiplier=0))
            one(pool.iota(INTS[:, E:E + NT], [[P, NT]], base=0, channel_multiplier=0))
            one(pool.iota(INTS[:, E + NT:], [[1, XS_TILES]], base=0, channel_multiplier=0))
            assert made == CONSTS

            pool.wait_ge(slots_ready, 1)
            pool.wait_ge(xs_zeroed, 64)
            for b in range(B + 1):
                if b < B:
                    for t in range(TB * b, TB * b + TB):
                        for k in range(2):
                            pool.indirect_dma_start(xs_dram, bass.IndirectOffsetOnAxis(IDX[:, k, t:t + 1], 0),
                                                    XN[:, t, :], None).then_inc(scattered[b], 16)
                if b > 0:
                    pool.wait_ge(scattered[b - 1], 16 * 2 * TB)
                    pool.sem_inc(xn_taken, 1)

            pool.wait_ge(phase_done, 3)
            with pool.Fori(0, XS_TILES // 2) as i:
                for k in range(2):
                    low_part(pool, 2 * i + k, k, 1)
            pool.wait_ge(low_ready[1], XS_TILES)
            pool.sem_inc(phase_done, 1)

            pool.wait_ge(y_stored, 1)
            pool.wait_ge(phase_done, 8)
            ov = out.rearrange("(t p) d -> p t d", p=P)
            step = Count()

            def link(ins):
                ins.then_inc(pool_step, 1)
                pool.wait_ge(pool_step, step.add())

            def gather(b):
                for t in range(b * TB, (b + 1) * TB):
                    for k in range(2):
                        pool.indirect_dma_start(YG[:, t, k, :], None, ys_dram,
                                                bass.IndirectOffsetOnAxis(IDX[:, k, t:t + 1], 0)
                                                ).then_inc(gathered[b], 16)

            def combine(b):
                rows = slice(b * TB, (b + 1) * TB)
                xr = XR[:, rows, :]
                pool.wait_ge(xr_in[b], 32 if b < B // 2 else 16)
                if b < B // 2:
                    total, first = XN, XN[:, rows, :]
                else:
                    total, first = XR, BOUT[:].unsqueeze(1).to_broadcast([P, TB, D])
                link(pool.tensor_tensor(out=total[:, rows, :], in0=xr, in1=first, op=ALU.add))
                pool.wait_ge(gathered[b], 16 * 2 * TB)
                y = YG[:, rows, :, :]
                weight = PW[:, :, rows].rearrange("p k t -> p t k").unsqueeze(3).to_broadcast([P, TB, 2, D])
                link(pool.tensor_tensor(out=y, in0=y, in1=weight, op=ALU.mult))
                for k in range(2):
                    link(pool.tensor_tensor(out=total[:, rows, :], in0=total[:, rows, :], in1=y[:, :, k, :], op=ALU.add))

            for i, b in enumerate(LAST_ORDER):
                if i == 0:
                    gather(b)
                if i + 1 < B:
                    gather(LAST_ORDER[i + 1])
                combine(b)
                if b < B // 2:
                    pool.dma_start(ov[:, b * TB:(b + 1) * TB, :], XN[:, b * TB:(b + 1) * TB, :]).then_inc(out_done, 16)
                else:
                    pool.sem_inc(rest_ready, 1)
            for b in range(B // 2, B - 1):
                pool.wait_ge(r_free, (b + 1) * NWIN + 1)
                pool.dma_start(ov[:, b * TB:(b + 1) * TB, :], XN[:, b * TB:(b + 1) * TB, :]).then_inc(out_done, 16)
            for t in range(NT - TB, NT):
                pool.wait_ge(r_free, t + 2)
                pool.dma_start(ov[:, t:t + 1, :], XN[:, t:t + 1, :]).then_inc(out_done, 16)

        @block.scalar
        def _(act):
            c = pair_counts()
            act.dma_start(GW, gate).then_inc(gate_in, 16)
            act.dma_start(WQKV[:], wqkv).then_inc(consts_in, 16)
            act.dma_start(BQK[:], bqk).then_inc(consts_in, 16)
            act.dma_start(BV, bv).then_inc(consts_in, 16)
            act.dma_start(WOUT[:], wout).then_inc(consts_in, 16)
            act.dma_start(BOUT[:], bout).then_inc(consts_in, 16)
            act.sem_inc(probs_ready, 2)
            act.sem_inc(ht_free, 1)

            def take_sqrt(g):
                act.wait_ge(var_ready, g + 1)
                act.activation(STD[:, 8 * g:8 * g + 8], VAR[:, 8 * g:8 * g + 8], ACT.Sqrt).then_inc(std_ready, 1)

            def take_part(blk, bk, full, n):
                if blk == 0:
                    wait_some(act, parts_out, c["NB"].now() * PARTS_OUT)
                    c["NB"].add()
                act.wait_ge(full, n)
                act.activation(PARTS[:, 0, blk, :], bk[:, 0:SPAN], ACT.Identity,
                               bias=BQK[:, blk:blk + 1]).then_inc(part0_ready, 1)

            take_sqrt(0)
            take_sqrt(1)
            for i in range(NT // 2):
                act.wait_ge(tok_full, i + 1)
                act.activation(XT[:, :, 2 * i * P:2 * (i + 1) * P],
                               TOK_BANK[i % 2].rearrange("p (c n) -> p c n", c=NC_D), ACT.Copy).then_inc(tok_free, 1)
                if i in (3, 7):
                    take_sqrt((i + 1) // 4 + 1)
                if i in FIRST_STEPS:
                    if i == FIRST_STEPS[0]:
                        act.wait_ge(consts_in, 80)
                    take_part(FIRST_STEPS.index(i), FIRST_BANK[FIRST_STEPS.index(i)], first_full, FIRST_STEPS.index(i) + 1)
                if i % 2 == 0 and i:
                    src = i // 2 - 1
                    act.wait_ge(tok_free, i)
                    for nb in (src, src + B):
                        if 0 < nb < B + 2:
                            act.dma_start(xt_dram[nb], XT[:, :, src * L:src * L + SPAN]).then_inc(xt_out, 16)
            act.wait_ge(tok_free, NT // 2)
            act.dma_start(xt_dram[B - 1], XT[:, :, (B - 1) * L:(B - 1) * L + SPAN]).then_inc(xt_out, 16)
            act.wait_ge(gap_ready, 1)
            act.activation(E2, PA, ACT.Exp).then_inc(e2_ready, 1)
            c["T"].add(1)

            def exps(u, q):
                act.wait_ge(st_full, c["ST"].add())
                act.activation(PT[:, 2 * (u % 2) + q, :], ST_BANK[q], ACT.Exp, scale=SCALE).then_inc(probs_ready, 1)

            def take_turned():
                act.wait_ge(t_full, c["T"].add())
                act.activation(OTS[:], T_BANK[:, 0:D].rearrange("p (c n) -> p c n", c=NC_D), ACT.Copy
                               ).then_inc(t_free, 1)

            def pair(stage):
                for par in range(2):
                    for u in range(UNITS):
                        if stage and u == 3:
                            act.wait_ge(y_stored, 1)
                        if u % 2 == 1 and u > 1:
                            take_turned()
                        c["T"].add(1)
                        if u < 4:
                            take_part(u, W_BANK, w_full, c["W"].add())
                        else:
                            c["W"].add(1)
                        if u < UNITS - 1:
                            exps(u + 1, 0)
                            exps(u + 1, 1)
                    exps(0, 0)
                    take_turned()
                    exps(0, 1)

            exps(0, 0)
            exps(0, 1)
            for stage in range(2):
                with loop(act, PAIRS, c["T"], c["W"], c["ST"], c["NB"]):
                    pair(stage)
                if stage:
                    break
                act.wait_ge(probs_ready, c["ST"].now() + 2)
                act.sem_inc(phase_done, 1)
                act.wait_ge(phase_done, 3)

                def take_tanh(j, k):
                    act.wait_ge(h1_full, j + 1)
                    act.activation(HID[:, k, :], bank(2 * k), ACT.Tanh, scale=0.5).then_inc(tanh_ready, 1)

                def take_ht(j):
                    act.wait_ge(ht_full, j + 1)
                    act.activation(HTS, bank(6).rearrange("p (c n) -> p c n", c=FC), ACT.Copy).then_inc(ht_free, 1)

                def take_xt(j, k):
                    act.wait_ge(xt_full, j + 1)
                    act.activation(XTS[:, k, 0], bank(4 + k)[:, 0:D].rearrange("p (c n) -> p c n", c=NC_D),
                                   ACT.Copy).then_inc(xt_high, 1)

                def high_part(j, k, half, used=None):
                    weights = weights_of(act, j, half)
                    if used is not None:
                        act.wait_ge((h1_full, h2_full)[half], used)
                    act.activation(WS[:, k, half, 0], weights, ACT.Copy
                                   ).then_inc(high_ready[half], 1)

                act.wait_ge(weights_in, 16 * E)
                act.wait_ge(rows_out, 16 * (B // 2))
                act.wait_ge(xn_taken, B)
                for j in range(2):
                    high_part(j, j, 0)
                    high_part(j, j, 1)
                    take_xt(j, j)
                take_tanh(0, 0)
                with act.Fori(0, SLOT_TILES // 2) as i:
                    for k in range(2):
                        j = 2 * i + k
                        high_part(j + 2, k, 0, j + 1)
                        take_tanh(j + 1, 1 - k)
                        take_ht(j)
                        high_part(j + 2, k, 1, j + 1)
                        take_xt(j + 2, k)
                take_ht(SLOT_TILES - 1)
                act.wait_ge(ht_free, SLOT_TILES + 1)
                act.wait_ge(high_ready[1], XS_TILES)
                act.sem_inc(phase_done, 1)
                act.wait_ge(phase_done, 8)

        @block.vector
        def _(dve):
            c = pair_counts()
            step = Count(0, 0)

            def link(ins):
                ins.then_inc(dve_step, 1)
                dve.wait_ge(dve_step, step.add())

            def tt(o, a, b, op):
                return dve.tensor_tensor(out=o, in0=a, in1=b, op=op)

            def ts(o, a, s1, s2, op0, op1):
                return dve.tensor_scalar(out=o, in0=a, scalar1=s1, scalar2=s2, op0=op0, op1=op1)

            def red(o, a, op, **kw):
                return dve.tensor_reduce(out=o, in_=a, axis=AX_X, op=op, **kw)

            def wide(v, n=E):
                return v.unsqueeze(2).to_broadcast([P, v.shape[1], n])

            for s in (o_free, r_free, w_free, ys_ready):
                dve.sem_inc(s, 1)
            dve.sem_inc(g_done, 2)
            dve.sem_inc(hid_done, 2)
            dve.sem_inc(xt_free, 2)

            def variance(g):
                lo, hi = 8 * g, 8 * g + 8
                dve.wait_ge(x_in[g], 16)
                for t in range(lo, hi):
                    dve.bn_stats(out=STAT[:, t, :], in_=XN[:, t, :]).then_inc(dve_step, 1)
                    step.add()
                dve.wait_ge(dve_step, step.now())
                me, mo = STAT[:, lo:hi, 1], STAT[:, lo:hi, 4]
                ve, vo = STAT[:, lo:hi, 2], STAT[:, lo:hi, 5]
                mean, var, dif, tmp = MEAN[:, lo:hi], VAR[:, lo:hi], DIF[:, lo:hi], TMP[:, lo:hi]
                tt(tmp, ve, vo, ALU.add).then_inc(dve_step, 1)
                step.add()
                tt(mean, me, mo, ALU.add).then_inc(dve_step, 1)
                step.add()
                link(tt(dif, me, mo, ALU.subtract))
                ts(mean, mean, 0.5, None, ALU.mult, ALU.bypass).then_inc(dve_step, 1)
                step.add()
                link(tt(dif, dif, dif, ALU.mult))
                link(ts(dif, dif, 0.25, EPS, ALU.mult, ALU.add))
                link(dve.scalar_tensor_tensor(out=var, in0=tmp, scalar=1.0 / D, in1=dif, op0=ALU.mult, op1=ALU.add))
                dve.sem_inc(var_ready, 1)

            def normalise(g):
                lo, hi = 8 * g, 8 * g + 8
                rs, var, tmp = RS[:, lo:hi], VAR[:, lo:hi], TMP[:, lo:hi]
                dve.wait_ge(std_ready, g + 1)
                link(dve.reciprocal(out=rs, in_=STD[:, lo:hi]))
                link(tt(tmp, rs, rs, ALU.mult))
                link(tt(tmp, tmp, var, ALU.mult))
                link(ts(tmp, tmp, -0.5, 1.5, ALU.mult, ALU.add))
                link(tt(rs, rs, tmp, ALU.mult))
                for t in range(lo, hi):
                    ts(XN[:, t, :], XN[:, t, :], MEAN[:, t:t + 1], RS[:, t:t + 1], ALU.subtract, ALU.mult
                       ).then_inc(xn_ready, 1)

            variance(0)
            for g in range(4):
                if g < 3:
                    variance(g + 1)
                normalise(g)

            dve.wait_ge(consts_made, CONSTS)
            dve.tensor_copy(REV, INTS[:, 0:E])
            dve.tensor_copy(TH, INTS[:, E:E + NT])
            link(dve.tensor_copy(JI, INTS[:, E + NT:]))
            dve.wait_ge(consts_in, 80)
            for k in range(NC_D):
                dve.tensor_copy(BVB[:, k, :], BV[:, k:k + 1].to_broadcast([P, P])).then_inc(bv_ready, 1)

            def split(blk, first=False):
                wait_some(dve, parts_ready, c["QK"].now())
                dve.wait_ge(part0_ready, c["QK"].add())
                dve.wait_ge(*((first_full, blk + 1) if first else (w_full, c["W"].add())))
                bk = FIRST_BANK[blk] if first else W_BANK
                rest = dve.scalar_tensor_tensor(out=REST, in0=bk[:, 0:SPAN], scalar=BQK[:, blk:blk + 1],
                                                in1=PARTS[:, 0, blk, :], op0=ALU.add, op1=ALU.subtract)
                if first:
                    link(rest)
                else:
                    rest.then_inc(w_free, 1)
                    dve.wait_ge(w_free, c["W"].now() + 1)
                link(dve.tensor_copy(PARTS[:, 1, blk, :], REST))
                tt(PARTS[:, 2, blk, :], REST, PARTS[:, 1, blk, :], ALU.subtract).then_inc(parts_ready, 1)

            def take_values(n):
                dve.wait_ge(w_full, c["W"].add())
                dve.tensor_copy(VW[:, n, :, 0:HD], W_BANK[:, 0:D].rearrange("p (h d) -> p h d", d=HD)
                                ).then_inc(w_free, 1)

            for blk in range(4):
                split(blk, True)

            def top(scores, most, one_hot):
                link(red(most, scores, ALU.max))
                link(tt(EQ, scores, wide(most), ALU.is_equal))
                link(tt(KEY, EQ, REV.unsqueeze(1).to_broadcast([P, NT, E]), ALU.mult))
                link(red(KM, KEY, ALU.max))
                link(tt(one_hot, KEY, wide(KM), ALU.is_equal))

            dve.wait_ge(gates_full, 1)
            link(dve.tensor_copy(G, bank(0)[:, 0:NT * E].rearrange("p (t e) -> p t e", e=E)))
            top(G, M1, OH1)
            link(dve.scalar_tensor_tensor(out=G2, in0=OH1, scalar=FAR, in1=G, op0=ALU.mult, op1=ALU.add))
            top(G2, M2, OH2)
            tt(MASK, OH1, OH2, ALU.add).then_inc(mask_ready, 1)
            tt(PA, M2, M1, ALU.subtract).then_inc(gap_ready, 1)

            dve.wait_ge(first_full, 4 + NWIN)
            for n in range(0, NWIN, 2):
                dve.tensor_copy(VW[:, n:n + 2, :, 0:HD], TOK_BANK[n // 2].rearrange("p (n h d) -> p n h d", n=2, d=HD)
                                ).then_inc(values_taken, 1)
            dve.wait_ge(bv_full, 1)
            link(tt(BOUT[:], BOUT[:], BV_BANK, ALU.add))

            dve.wait_ge(ranks_full, 1)
            ps_rank = bank(1)[:, 0:NT * E].rearrange("p (t e) -> p t e", e=E)
            ps_tot = bank(1)[:, NT * E:2 * NT * E].rearrange("p (t e) -> p e t", e=E)
            tot, inc, exc = (v.rearrange("p (e t) -> p e t", e=E) for v in (TOT, INC, EXC))
            link(dve.tensor_copy(RANK, ps_rank))
            link(dve.tensor_copy(tot, ps_tot))
            dve.sem_inc(ranks_taken, 1)
            link(dve.tensor_tensor_scan(out=INC, data0=RMASK, data1=TOT, initial=0.0, op0=ALU.mult, op1=ALU.add))
            link(tt(EXC, INC, TOT, ALU.subtract))
            link(tt(CMP, inc[:, :, NT - 1:NT].to_broadcast([P, E, NT]), TH.unsqueeze(1).to_broadcast([P, E, NT]),
                    ALU.is_gt))
            link(red(NTL, CMP, ALU.add))
            link(dve.tensor_tensor_scan(out=INCT, data0=ONE8, data1=NTL, initial=0.0, op0=ALU.mult, op1=ALU.add))
            link(tt(BASE, INCT, NTL, ALU.subtract))
            link(ts(BASE, BASE, float(P), None, ALU.mult, ALU.bypass))
            link(tt(SLOT, RANK, exc.rearrange("p e t -> p t e"), ALU.add))
            link(tt(SLOT, SLOT, BASE.unsqueeze(1).to_broadcast([P, NT, E]), ALU.add))
            for k, one_hot in enumerate((OH1, OH2)):
                link(tt(PICK, SLOT, one_hot, ALU.mult))
                link(red(SLOTF[:, k, :], PICK, ALU.add))
            dve.tensor_copy(IDX[:], SLOTF).then_inc(slots_ready, 1)
            link(tt(CMPJ, INCT.unsqueeze(1).to_broadcast([P, XS_TILES, E]), wide(JI), ALU.is_le))
            link(red(EJF, CMPJ, ALU.add))
            link(ts(EJF, EJF, float(E - 1), None, ALU.min, ALU.bypass))
            link(dve.tensor_copy(EJ[:], EJF[0:1, :]))
            dve.wait_ge(e2_ready, 1)
            link(ts(M1, E2, 1.0, None, ALU.add, ALU.bypass))
            link(dve.reciprocal(out=M2, in_=M1))
            link(ts(PW[:, 0, :], M2, 0.5, None, ALU.mult, ALU.bypass))
            link(dve.scalar_tensor_tensor(out=PW[:, 1, :], in0=E2, scalar=0.5, in1=M2, op0=ALU.mult, op1=ALU.mult))
            dve.sem_inc(temps_done, 1)

            def take_max():
                wait_some(dve, mh_ready, c["S"].now())
                dve.wait_ge(s_full, c["S"].add())
                red(MNEG[:], S_BANKS.rearrange("p (h k) -> p h k", k=WIN), ALU.max, negate=True).then_inc(s_free, 1)
                dve.wait_ge(s_free, c["S"].now())
                link(dve.tensor_copy(MH[:, 0:HH], MNEG[:]))
                tt(MH[:, HH:2 * HH], MNEG[:], MH[:, 0:HH], ALU.subtract).then_inc(mh_ready, 1)

            def take_negm(k):
                dve.wait_ge(t_full, c["T"].add())
                dve.tensor_copy(NEGM[:, k, :], T_BANK[0:STK, 0:P // 2].bitcast(BF16)).then_inc(t_free, 1)

            take_max()
            take_negm(0)
            take_max()

            def norm():
                dve.wait_ge(o_free, c["O"].now() + 1)
                dve.wait_ge(o_full, c["O"].add())
                o = O_BANK[:, 0:H * (HD + 1)].rearrange("p (h d) -> p h d", d=HD + 1)
                link(dve.reciprocal(out=RDEN[:], in_=o[:, :, HD]))
                tt(OSB[:], o[:, :, 0:HD], RDEN[:].unsqueeze(2).to_broadcast([P, H, HD]), ALU.mult
                   ).then_inc(o_free, 1)

            def row(t, of=XN):
                return of[:, bass.ds(t, 1), :].rearrange("p o d -> p (o d)")

            def project(stage, b, n):
                dve.wait_ge(r_full, c["R"].add())
                rest = row(b * TB + n, XR) if stage else BOUT[:]
                tt(row(b * TB + n), R_BANK[:, 0:D], rest, ALU.add).then_inc(r_free, 1)

            for stage in range(2):
                step.per = PAIR_STEPS
                with loop(dve, PAIRS, step, c["T"], c["W"], c["S"], c["O"], c["R"], c["QK"]) as i:
                    for par in range(2):
                        b = 4 * stage + 2 * i + par
                        for u in range(UNITS):
                            if u % 2 == 1 and u > 1:
                                c["T"].add(1)
                            take_negm((u + 1) % 2)
                            if u < 4:
                                split(u)
                            elif u < 6:
                                take_values(u - 4)
                            if stage and u == 2:
                                dve.wait_ge(y_stored, 1)
                            if u % 2 == 0 and u > 1:
                                norm()
                            if u == 6:
                                take_values(2)
                            take_max()
                            if u == 3:
                                dve.wait_ge(xn_taken, b + 1)
                                if stage:
                                    dve.wait_ge(rest_ready, 2 * i + par + 1)
                            if u % 2 == 1 and u > 1:
                                project(stage, b, u // 2 - 1)
                        norm()
                        take_values(3)
                        c["T"].add(1)
                        project(stage, b, NWIN - 1)
                if stage:
                    break
                dve.wait_ge(r_free, c["R"].now() + 1)
                dve.sem_inc(phase_done, 1)
                dve.wait_ge(phase_done, 3)

                def hidden(j, k):
                    dve.wait_ge(tanh_ready, j + 1)
                    dve.scalar_tensor_tensor(out=HID[:, k, :], in0=HID[:, k, :], scalar=1.0, in1=bank(2 * k),
                                             op0=ALU.add, op1=ALU.mult).then_inc(g_done, 1)
                    dve.wait_ge(g_done, j + 3)
                    dve.wait_ge(h2_full, j + 1)
                    tt(HID[:, k, :], HID[:, k, :], bank(2 * k + 1), ALU.mult).then_inc(hid_done, 1)

                def take_y(j, k, stored):
                    dve.wait_ge(y_full, j + 1)
                    wait_some(dve, y_out[k], 16 * stored)
                    dve.tensor_copy(YS[k], bank(7)[:, 0:D]).then_inc(ys_ready, 1)

                def low_xt(j, k):
                    dve.wait_ge(xt_high, j + 1)
                    tt(XTS[:, k, 1], bank(4 + k)[:, 0:D].rearrange("p (c n) -> p c n", c=NC_D),
                       XTS[:, k, 0].bitcast(F32), ALU.subtract).then_inc(xt_free, 1)

                for j in range(2):
                    low_part(dve, j, j, 0)
                    low_xt(j, j)
                hidden(0, 0)
                for k in range(2):
                    low_part(dve, k + 2, k, 0)
                    hidden(k + 1, 1 - k)
                    low_xt(k + 2, k)
                    take_y(k, k, 0)
                with dve.Fori(1, SLOT_TILES // 2) as i:
                    for k in range(2):
                        low_part(dve, 2 * i + k + 2, k, 0)
                        hidden(2 * i + k + 1, 1 - k)
                        low_xt(2 * i + k + 2, k)
                        take_y(2 * i + k, k, i)
                take_y(SLOT_TILES - 1, (SLOT_TILES - 1) % 2, SLOT_TILES // 2)
                dve.wait_ge(ys_ready, SLOT_TILES)
                dve.sem_inc(phase_done, 1)
                dve.wait_ge(phase_done, 8)

        @block.tensor
        def _(pe):
            c = pair_counts()

            def mm(o, a, b, start=True, stop=True):
                return pe.matmul(o, a, b, start=start, stop=stop)

            def project_block(o, blk, xt, full):
                for ch in range(NC_D):
                    last = mm(o, WQKV[:, ch, blk * P:(blk + 1) * P], xt[:, ch, 0:SPAN], ch == 0, ch == NC_D - 1)
                last.then_inc(full, 1)

            def project_values(o, n, xt, full):
                for ch in range(NC_D):
                    last = mm(o, xt[:, ch, n * STRIDE:n * STRIDE + WIN], WQKV[:, ch, 2 * D:3 * D],
                              ch == 0, ch == NC_D - 1)
                last.then_inc(full, 1)

            pe.wait_ge(consts_made, 2)

            def turn_pair(i):
                pe.wait_ge(xn_ready, 2 * i + 2)
                if i > 1:
                    pe.wait_ge(tok_free, i - 1)
                for ch in range(NC_D):
                    for k in range(2):
                        last = pe.transpose(TOK_BANK[i % 2][:, (2 * ch + k) * P:(2 * ch + k + 1) * P],
                                            XN[:, 2 * i + k, ch * P:(ch + 1) * P], IDF[:])
                last.then_inc(tok_full, 1)

            def score_pair(i):
                pe.wait_ge(tok_free, i + 1)
                for t in (2 * i, 2 * i + 1):
                    for ch in range(NC_D):
                        last = mm(bank(0)[:, t * E:(t + 1) * E], XT[:, ch, t * P:(t + 1) * P], GW[:, ch, :],
                                  ch == 0, ch == NC_D - 1)
                return last

            turn_pair(0)
            pe.wait_ge(gate_in, 16)
            for i in range(1, NT // 2):
                turn_pair(i)
                score_pair(i - 1)
                if i == FIRST_STEPS[0]:
                    pe.wait_ge(consts_in, 80)
                if i in FIRST_STEPS:
                    blk = FIRST_STEPS.index(i)
                    project_block(FIRST_BANK[blk][:, 0:SPAN], blk, XT, first_full)
            pe.wait_ge(bv_ready, NC_D)
            for ch in range(NC_D):
                last = mm(BV_BANK, BVB[:, ch, :], WOUT[:, ch, :], ch == 0, ch == NC_D - 1)
            last.then_inc(bv_full, 1)
            score_pair(NT // 2 - 1).then_inc(gates_full, 1)
            for n in range(NWIN):
                project_values(TOK_BANK[n // 2][:, (n % 2) * D:(n % 2 + 1) * D], n, XT, first_full)

            def queries_keys(blk):
                pe.wait_ge(w_free, c["W"].now() + 1)
                project_block(W_BANK[:, 0:SPAN], blk, XNT, w_full)
                c["W"].add()

            def values(n):
                pe.wait_ge(w_free, c["W"].now() + 1)
                project_values(W_BANK[:, 0:D], n, XNT, w_full)
                c["W"].add()

            pe.wait_ge(consts_made, CONSTS)
            pe.wait_ge(mask_ready, 1)
            mm(bank(1)[:, 0:NT * E], BEFORE, MASK.rearrange("p t e -> p (t e)"))
            mm(bank(1)[:, NT * E:2 * NT * E], ONES, MASK.rearrange("p t e -> p (t e)")).then_inc(ranks_full, 1)

            def scores(par, u):
                n, half = u // 2, u % 2
                wait_some(pe, s_free, c["S"].now())
                w = slice(n * STRIDE, n * STRIDE + WIN)
                for h in range(HH):
                    last = mm(S_BANKS[:, h * WIN:(h + 1) * WIN], QS[:, par, half * HH + h, w],
                              KS[:, par, half * HH + h, w])
                last.then_inc(s_full, 1)
                c["S"].add()

            def shift_row():
                pe.wait_ge(mh_ready, c["S"].now())
                wait_some(pe, t_free, c["T"].now())
                pe.transpose(T_BANK[0:STK, 0:P // 2].bitcast(BF16), MH[:], IDB[:]).then_inc(t_full, 1)
                c["T"].add()

            def shifted(par, u):
                n, half = u // 2, u % 2
                w = slice(n * STRIDE, n * STRIDE + WIN)
                pe.wait_ge(t_free, c["T"].now())
                for q in range(2):
                    pe.wait_ge(probs_ready, c["ST"].now() + 1)
                    for hq in range(HQ):
                        h = q * HQ + hq
                        o = ST_BANK[q][:, hq * WIN:(hq + 1) * WIN]
                        mm(o, KS[:, par, half * HH + h, w], QS[:, par, half * HH + h, w], True, False)
                        last = mm(o, SEL[:, h, :], NEGM[:, u % 2, :], False, True)
                    last.then_inc(st_full, 1)
                    c["ST"].add()

            def weighted(u, behind):
                n, half = u // 2, u % 2
                if half == 0:
                    pe.wait_ge(o_free, c["O"].now() + 1)
                pe.wait_ge(probs_ready, c["ST"].now() + 2 - behind)
                for h in range(HH):
                    hh = half * HH + h
                    last = mm(O_BANK[:, hh * (HD + 1):(hh + 1) * (HD + 1)],
                              PT[:, 2 * (u % 2) + h // HQ, (h % HQ) * WIN:(h % HQ + 1) * WIN], VW[:, n, hh, :])
                if half:
                    last.then_inc(o_full, 1)
                    c["O"].add()

            def turn():
                pe.wait_ge(o_free, c["O"].now() + 1)
                pe.wait_ge(t_free, c["T"].now())
                for ch in range(NC_D):
                    last = pe.transpose(T_BANK[:, ch * P:(ch + 1) * P],
                                        OSB[:].rearrange("p h d -> p (h d)")[:, ch * P:(ch + 1) * P], IDF[:])
                last.then_inc(t_full, 1)
                c["T"].add()

            def project(tfree):
                pe.wait_ge(t_free, tfree)
                pe.wait_ge(r_free, c["R"].now() + 1)
                for ch in range(NC_D):
                    last = mm(R_BANK[:, 0:D], OTS[:, ch, :], WOUT[:, ch, :], ch == 0, ch == NC_D - 1)
                last.then_inc(r_full, 1)
                c["R"].add()

            pe.wait_ge(stack_in[0], 2 * NLEV * 16)
            pe.wait_ge(ranks_taken, 1)
            pe.wait_ge(values_taken, NWIN // 2)
            scores(0, 0)
            shift_row()
            scores(0, 1)
            shifted(0, 0)
            loads = Count(2 * NLEV * 16, 2 * NLEV * 16)

            for stage in range(2):
                with loop(pe, PAIRS, c["T"], c["W"], c["S"], c["ST"], c["O"], c["R"], loads) as i:
                    for par in range(2):
                        b = 2 * i + (4 * stage + par)
                        for u in range(UNITS):
                            if u % 2 == 1 and u > 1:
                                turn()
                            if u == 0:
                                pe.wait_ge(xnt_in, b * 16 + 16)
                            if u < 4:
                                queries_keys(u)
                            else:
                                values(u - 4)
                            shift_row()
                            if u > 0:
                                weighted(u - 1, 2)
                            if u < UNITS - 2:
                                scores(par, u + 2)
                            else:
                                if u == UNITS - 2:
                                    if par == 1:
                                        loads.add(2 * NLEV * 16)
                                    pe.wait_ge(stack_in[1 - par], loads.now())
                                scores(1 - par, u + 2 - UNITS)
                            if u < UNITS - 1:
                                shifted(par, u + 1)
                            if u % 2 == 1 and u > 1:
                                project(c["T"].now(1))
                        weighted(UNITS - 1, 0)
                        shifted(1 - par, 0)
                        turn()
                        project(c["T"].now())
                if stage:
                    break
                pe.wait_ge(r_full, c["R"].now())
                pe.sem_inc(phase_done, 1)
                pe.wait_ge(phase_done, 3)
                pe.wait_ge(weights_in, 16 * E)

                def tokens(j, k):
                    pe.wait_ge(xs_in[k], (j - k) * 8 + 16)
                    pe.wait_ge(xt_free, j + 1)
                    for ch in range(NC_D):
                        last = pe.transpose(bank(4 + k)[:, ch * P:(ch + 1) * P], XS[:, k, ch * P:(ch + 1) * P], IDF[:])
                    last.then_inc(xt_full, 1)

                def up(j, k, half):
                    full, free = ((h1_full, g_done), (h2_full, hid_done))[half]
                    if half == 0:
                        pe.wait_ge(xt_free, j + 3)
                    pe.wait_ge(low_ready[half], j + 1)
                    pe.wait_ge(free, j + 1)
                    n = 0
                    for ch in range(NC_D):
                        for lx, lw in ((0, 0), (0, 1), (1, 0)):
                            last = mm(bank(2 * k + half), XTS[:, k, lx, ch, :],
                                      WS[:, k, half, lw, ch, :], n == 0, n == 3 * NC_D - 1)
                            n += 1
                    last.then_inc(full, 1)

                def turn_hidden(j, k):
                    pe.wait_ge(hid_done, j + 3)
                    pe.wait_ge(ht_free, j + 1)
                    for f in range(FC):
                        last = pe.transpose(bank(6)[:, f * P:(f + 1) * P], HID[:, k, f * P:(f + 1) * P], IDF[:])
                    last.then_inc(ht_full, 1)

                def down(j, at):
                    pe.wait_ge(ht_free, j + 2)
                    pe.wait_ge(ys_ready, j + 1)
                    for f in range(FC):
                        last = mm(bank(7)[:, 0:D], HTS[:, f, :],
                                  WALL[:, bass.ds(at + 2 * NC_D * FH + f * D, D)], f == 0, f == FC - 1)
                    last.then_inc(y_full, 1)

                def expert(j):
                    return pe.value_load(EJ[0:1, bass.ds(j, 1)], min_val=0, max_val=E - 1) * WE

                tokens(0, 0)
                tokens(1, 1)
                up(0, 0, 0)
                up(0, 0, 1)
                with pe.Fori(0, SLOT_TILES // 2) as i:
                    for k in range(2):
                        j = 2 * i + k
                        up(j + 1, 1 - k, 0)
                        at = expert(j)
                        turn_hidden(j, k)
                        up(j + 1, 1 - k, 1)
                        tokens(j + 2, k)
                        down(j, at)
                j = SLOT_TILES - 1
                turn_hidden(j, j % 2)
                down(j, expert(j))
                pe.wait_ge(y_full, SLOT_TILES)
                pe.sem_inc(phase_done, 1)
                pe.wait_ge(phase_done, 8)


_NAMES = ("L0_attn_x", "L0_attn_w_qkv", "L0_attn_b_qkv", "L0_attn_w_out", "L0_attn_b_out", "L0_ffn_w12", "L0_ffn_w3",
          "L0_ffn_gate_w")


def kernel(**inputs):
    import numpy as np
    import concourse.bacc as bacc
    from concourse.bass_utils import run_bass_kernel_spmd

    x, w_qkv, b_qkv, w_out, b_out, w12, w3, gate_w = (np.asarray(inputs[n]) for n in _NAMES)

    def down(w):
        return w.reshape(-1, P, w.shape[-1]).transpose(1, 0, 2).reshape(P, -1)

    w12_t = w12.transpose(0, 2, 1).reshape(E, NC_D, P, 2 * FH).transpose(2, 0, 1, 3).reshape(P, E, -1)
    w3_t = w3.transpose(0, 2, 1).reshape(E, FC, P, D).transpose(2, 0, 1, 3).reshape(P, E, -1)
    arrays = {
        "x": x.reshape(B * L, D),
        "wqkv": down(w_qkv),
        "bqk": b_qkv[:2 * D].reshape(4, P).T,
        "bv": b_qkv[2 * D:].reshape(NC_D, P).T,
        "wout": down(w_out),
        "bout": np.broadcast_to(b_out, (P, D)),
        "gate": down(gate_w.T),
        "wexp": np.concatenate([w12_t, w3_t], axis=2).reshape(P, E * WE),
    }
    arrays = {f"in_{k}": np.ascontiguousarray(v) for k, v in arrays.items()}
    nc = bacc.Bacc("TRN2", target_bir_lowering=False, num_devices=1)
    args = [nc.dram_tensor(k, v.shape, mybir.dt.from_np(v.dtype), kind="ExternalInput").ap()
            for k, v in arrays.items()]
    args.append(nc.dram_tensor("out_0", (B * L, D), F32, kind="ExternalOutput").ap())
    layer(nc, *args)
    r = run_bass_kernel_spmd(nc, [arrays], core_ids=[0])
    return r.results[0]["out_0"].reshape(B, L, D)
```

```python
from contextlib import ExitStack, contextmanager

import concourse.bass as bass
from concourse import mybir

F32 = mybir.dt.float32
BF16 = mybir.dt.bfloat16
F32R = mybir.dt.float32r
I32 = mybir.dt.int32
U32 = mybir.dt.uint32
ALU = mybir.AluOpType
ACT = mybir.ActivationFunctionType
AX_X = mybir.AxisListType.X

P = 128
B, L, D = 8, 512, 256
NC_D = D // P
TB = L // P
NT = B * TB
H, HD = 16, 16
WIN, STRIDE = 128, 64
NWIN = L // WIN
SPAN = STRIDE * (NWIN - 1) + WIN
HH = H // 2
UNITS = 2 * NWIN
HQ = HH // 2
SCALE = float(HD) ** -0.5
E, FH = 8, 512
FC = FH // P
SLOT_TILES = (2 * B * L + E * (P - 1)) // P
XS_TILES = SLOT_TILES + 1
XS_LOADS = XS_TILES + 1
WE = NC_D * 2 * FH + FC * D
EPS = 1e-5
BANK = 512
FAR = -3.0e38
Q_LEVELS = (0, 0, 1, 0, 2, 1)
K_LEVELS = (0, 1, 0, 2, 0, 1)
NLEV = len(Q_LEVELS)
STK = NLEV * HD
NPART = 3
PARTS_OUT = 4 * NPART * 16
PAIRS = 2


class Count:

    def __init__(self, start=0, per=0):
        self.base, self.n, self.per = start, 0, per

    def add(self, k=1):
        self.n += k
        return self.base + self.n

    def now(self, less=0):
        return self.base + (self.n - less)


@contextmanager
def loop(eng, times, *counts):
    starts = [c.now() for c in counts]
    with eng.Fori(0, times) as i:
        for c, s in zip(counts, starts):
            c.base, c.n = i * c.per + s, 0
        yield i
        for c in counts:
            assert c.n == c.per, (c.n, c.per)
    for c, s in zip(counts, starts):
        c.base, c.n = s + times * c.per, 0


def wait_some(eng, sem, value):
    if not (isinstance(value, int) and value == 0):
        eng.wait_ge(sem, value)


def layer(nc, x, wqkv, bqk, bv, wout, bout, gate, wexp, out):
    with ExitStack() as ctx:
        def sb(name, shape, dt=F32):
            return ctx.enter_context(nc.sbuf_tensor(name, shape, dt))

        def shared(name, shape, dt):
            with nc.sbuf_tensor(name, shape, dt) as buffer:
                return buffer

        def sem(name):
            return ctx.enter_context(nc.semaphore(name))

        xs_dram = nc.dram_tensor("xs_scratch", (XS_LOADS * P, D), F32, kind="Internal").ap()
        ys_dram = nc.dram_tensor("ys_scratch", (SLOT_TILES * P, D), F32, kind="Internal").ap()
        pd_dram = nc.dram_tensor("parts_scratch", (B + 1, NPART, 2, H, HD, SPAN), BF16, kind="Internal").ap()
        xt_dram = nc.dram_tensor("xt_scratch", (B + 2, P, NC_D, SPAN), F32, kind="Internal").ap()
        rows_dram = nc.dram_tensor("rows_scratch", (B // 2 * L, D), F32, kind="Internal").ap()

        WS = shared("WS", [P, 2, 2, 2, NC_D, FH], F32R)
        XN = sb("XN", [P, NT, D])
        WALL = sb("WALL", [P, E * WE])
        QS = sb("QS", [STK, 2, H, SPAN], BF16)
        KS = sb("KS", [STK, 2, H, SPAN], BF16)
        XTS = shared("XTS", [P, 2, 2, NC_D, P], F32R)
        WORK = sb("WORK", [P, 4928])
        VW = sb("VW", [P, NWIN, H, HD + 1])
        WQKV = sb("WQKV", [P, NC_D, 3 * D])
        WOUT = sb("WOUT", [P, NC_D, D])
        BOUT = sb("BOUT", [P, D])
        BQK = sb("BQK", [P, 4])
        IDF = sb("IDF", [P, P])
        IDB = sb("IDB", [P, P], BF16)
        SEL = sb("SEL", [STK, HH, P], BF16)
        OSB = sb("OSB", [P, H, HD])
        OTS = sb("OTS", [P, NC_D, P])
        MNEG = sb("MNEG", [P, HH])
        MH = sb("MH", [P, STK], BF16)
        NEGM = sb("NEGM", [STK, 2, P], BF16)
        RDEN = sb("RDEN", [P, H])
        PW = sb("PW", [P, 2, NT])
        IDX = sb("IDX", [P, 2, NT], U32)
        EJ = sb("EJ", [1, XS_TILES], I32)

        nq = 4 * SPAN // 2
        PARTS = WORK[:, 0:NPART * nq].bitcast(BF16).rearrange("p (l k t) -> p l k t", l=NPART, k=4)
        at = NPART * nq
        REST = WORK[:, at:at + SPAN]
        at += SPAN
        XNT = WORK[:, at:at + NC_D * SPAN].rearrange("p (c t) -> p c t", c=NC_D)
        at += NC_D * SPAN
        PT = WORK[:, at:at + 4 * BANK].rearrange("p (r n) -> p r n", r=4)
        assert at + 4 * BANK <= 4928
        at = 0

        def work(n):
            nonlocal at
            at += n
            assert at <= 4928
            return WORK[:, at - n:at]

        work(4 * D)
        XS = work(2 * D).rearrange("p (b n) -> p b n", b=2)
        HTS = work(FH).rearrange("p (c n) -> p c n", c=FC)
        assert at <= NPART * nq + SPAN
        at = NPART * nq + 3 * SPAN + 2 * BANK
        HID = work(2 * FH).rearrange("p (b n) -> p b n", b=2)
        YS = (OSB[:].rearrange("p h d -> p (h d)"), OTS[:].rearrange("p c n -> p (c n)"))
        at = 0

        def temp(n, dt=F32):
            nonlocal at
            at += n
            assert at <= E * WE
            v = WALL[:, at - n:at]
            return v if dt == F32 else v.bitcast(dt)

        ZERO = temp(XS_LOADS * D // 4)
        XT = temp(NC_D * NT * P).rearrange("p (c n) -> p c n", c=NC_D)
        GW = temp(NC_D * E).rearrange("p (c e) -> p c e", c=NC_D)
        BV = temp(NC_D)
        BVB = temp(NC_D * P).rearrange("p (c n) -> p c n", c=NC_D)
        BEFORE = temp(P)
        ONES = temp(P)
        STAT = temp(NT * 6).rearrange("p (t s) -> p t s", s=6)
        MEAN, VAR, DIF, STD, RS, TMP = (temp(NT) for _ in range(6))
        G, EQ, KEY, OH1, G2, OH2, MASK, RANK, SLOT, PICK = (
            temp(NT * E).rearrange("p (t e) -> p t e", e=E) for _ in range(10))
        TOT, INC, EXC, RMASK = (temp(NT * E) for _ in range(4))
        M1, KM, M2, E2, PA = (temp(NT) for _ in range(5))
        REV, NTL, INCT, BASE = (temp(E) for _ in range(4))
        ONE8 = temp(E)
        TH = temp(NT)
        CMP = temp(E * NT).rearrange("p (e t) -> p e t", e=E)
        JI = temp(XS_TILES)
        CMPJ = temp(XS_TILES * E).rearrange("p (j e) -> p j e", e=E)
        EJF = temp(XS_TILES)
        INTS = temp(E + NT + XS_TILES, I32)
        SLOTF = temp(2 * NT).rearrange("p (k t) -> p k t", k=2)
        assert 2 * NT * D + NT * D == E * WE
        YG = WALL[:, 0:2 * NT * D].rearrange("p (t k d) -> p t k d", k=2, d=D)
        XR = WALL[:, 2 * NT * D:].rearrange("p (t d) -> p t d", d=D)

        PS = ctx.enter_context(nc.psum_tensor("PS", [P, 8 * BANK], F32))

        def bank(k, n=1):
            return PS[:, k * BANK:(k + n) * BANK]

        S_BANKS = bank(0, 2)
        ST_BANK = (bank(2), bank(3))
        O_BANK, T_BANK, W_BANK, R_BANK = bank(4), bank(5), bank(6), bank(7)
        TOK_BANK = (bank(5), bank(6))
        FIRST_BANK = (bank(2), bank(3), bank(4), bank(7))
        FIRST_STEP = NT // 4
        BV_BANK = bank(1)[:, NT * E:NT * E + D]
        HALF = NT // 2

        x_in = [sem(f"x_in{g}") for g in range(4)]
        gate_in = sem("gate_in")
        consts_in = sem("consts_in")
        consts_made = sem("consts_made")
        zero_made = sem("zero_made")
        xs_zeroed = sem("xs_zeroed")
        var_ready = sem("var_ready")
        std_ready = sem("std_ready")
        xn_ready = sem("xn_ready")
        tok_full, tok_free = sem("tok_full"), sem("tok_free")
        gates_full = sem("gates_full")
        first_full = sem("first_full")
        values_taken = sem("values_taken")
        temps_done = sem("temps_done")
        xt_out = sem("xt_out")
        xnt_in = sem("xnt_in")
        bv_ready, bv_full = sem("bv_ready"), sem("bv_full")
        mask_ready = sem("mask_ready")
        ranks_full, ranks_taken = sem("ranks_full"), sem("ranks_taken")
        gap_ready = sem("gap_ready")
        e2_ready = sem("e2_ready")
        bases_ready = sem("bases_ready")
        scattered = [sem(f"scattered{b}") for b in range(B)]
        xn_taken = sem("xn_taken")
        t_full, t_free = sem("t_full"), sem("t_free")
        w_full, w_free = sem("w_full"), sem("w_free")
        s_full, s_free = sem("s_full"), sem("s_free")
        mh_ready = sem("mh_ready")
        st_full, probs_ready = sem("st_full"), sem("probs_ready")
        o_full, o_free = sem("o_full"), sem("o_free")
        r_full, r_free = sem("r_full"), sem("r_free")
        part0_ready = sem("part0_ready")
        parts_ready = sem("parts_ready")
        parts_out = sem("parts_out")
        stack_in = [sem("stack_in0"), sem("stack_in1")]
        weights_in = sem("weights_in")
        phase_done = sem("phase_done")
        y_stored = sem("y_stored")
        xs_in = [sem("xs_in0"), sem("xs_in1")]
        xt_full, xt_high, xt_free = sem("xt_full"), sem("xt_high"), sem("xt_free")
        rows_out = [sem("rows_out0"), sem("rows_out1")]
        high_ready = [sem("high_ready0"), sem("high_ready1")]
        low_ready = [sem("low_ready0"), sem("low_ready1")]
        h1_full, tanh_ready, g_done = sem("h1_full"), sem("tanh_ready"), sem("g_done")
        h2_full, hid_done = sem("h2_full"), sem("hid_done")
        ht_full, ht_free = sem("ht_full"), sem("ht_free")
        y_full, ys_ready = sem("y_full"), sem("ys_ready")
        y_out = [sem("y_out0"), sem("y_out1")]
        gathered = [[sem(f"gathered{half}_{b}") for b in range(B)] for half in range(2)]
        x_back = [sem(f"x_back{k}") for k in range(3)]
        rows_back = sem("rows_back")
        rest_ready = sem("rest_ready")
        pool_step = sem("pool_step")
        out_done, late_out = sem("out_done"), sem("late_out")
        dve_step = sem("dve_step")

        block = ctx.enter_context(nc.Block())

        def pair_counts():
            return dict(T=Count(0, 2 * (UNITS + NWIN)), W=Count(0, 2 * 8), S=Count(0, 2 * UNITS),
                        ST=Count(0, 4 * UNITS), O=Count(0, 2 * NWIN), R=Count(0, 2 * NWIN),
                        NB=Count(0, 2), QK=Count(0, 8))

        CONSTS = 17
        PAIR_STEPS = 2 * (UNITS + NWIN + 4)
        LAST_ORDER = (4, 5, 0, 6, 1, 7, 2, 3)
        assert sorted(LAST_ORDER) == list(range(B))

        def weights_of(eng, j, half):
            at = eng.value_load(EJ[0:1, bass.ds(j, 1)], min_val=0, max_val=E - 1) * WE
            return WALL[:, bass.ds(at, 2 * NC_D * FH)].rearrange("p (c h n) -> p c h n", c=NC_D, h=2)[:, :, half, :]

        def low_part(eng, j, k, half):
            weights = weights_of(eng, j, half)
            eng.wait_ge(high_ready[half], j + 1)
            eng.tensor_tensor(out=WS[:, 1 - k, half, 1], in0=weights, in1=WS[:, 1 - k, half, 0].bitcast(F32),
                              op=ALU.subtract).then_inc(low_ready[half], 1)

        @block.sync
        def _(sp):
            xv = x.rearrange("(t p) d -> p t d", p=P)
            for g in range(4):
                sp.dma_start(XN[:, 8 * g:8 * g + 8, :], xv[:, 8 * g:8 * g + 8, :]).then_inc(x_in[g], 16)
            sp.wait_ge(zero_made, 1)
            zv = xs_dram.rearrange("(p r) d -> p (r d)", p=P)
            q = XS_LOADS * D // 4
            for g in range(4):
                sp.dma_start(zv[:, g * q:(g + 1) * q], ZERO).then_inc(xs_zeroed, 16)

            def stacks(nb, par, at_once=False):
                def of(l, k):
                    return pd_dram[bass.ds(nb, 1), l, k].rearrange("o h d t -> (o h d) t")

                def out_(k):
                    for blk in (2 * k, 2 * k + 1):
                        sp.wait_ge(parts_ready, nb * 4 + (blk + 1))
                        for l in range(NPART):
                            sp.dma_start(of(l, k)[(blk % 2) * P:(blk % 2 + 1) * P], PARTS[:, l, blk, :]
                                         ).then_inc(parts_out, 16)

                def back(k, stack, levels):
                    sp.wait_ge(parts_out, nb * PARTS_OUT + (2 if at_once else k + 1) * (PARTS_OUT // 2))
                    for l in range(NLEV):
                        sp.dma_start(stack[HD * l:HD * l + HD, par],
                                     of(levels[l], k).rearrange("(h d) t -> d h t", d=HD)).then_inc(stack_in[par], 16)

                out_(0)
                if at_once:
                    out_(1)
                back(0, QS, Q_LEVELS)
                if not at_once:
                    out_(1)
                back(1, KS, K_LEVELS)

            stacks(0, 0, at_once=True)

            def load_tokens(b, first=False):
                if not first:
                    sp.wait_ge(w_full, b * 8)
                sp.dma_start(XNT, xt_dram[bass.ds(b + 1, 1)].rearrange("o p c t -> (o p) c t")).then_inc(xnt_in, 16)

            sp.wait_ge(xt_out, 16 * (B + 1))
            load_tokens(0, True)
            sp.wait_ge(temps_done, 2)
            sp.wait_ge(first_full, 4 + NWIN)
            sp.wait_ge(xs_zeroed, 64)
            for stage in range(2):
                with sp.Fori(0, PAIRS) as i:
                    for par in range(2):
                        b = 2 * i + (4 * stage + par)
                        sp.wait_ge(r_free, b * NWIN + 1)
                        def weights(k):
                            w = bass.ds(b * (2 * WE) + k * WE, WE)
                            sp.dma_start(WALL[:, w], wexp[:, w]).then_inc(weights_in, 16)

                        stacks(b + 1, 1 - par)
                        if stage == 0:
                            weights(0)
                            weights(1)
                        load_tokens(b + 1)
                        if stage:
                            sp.wait_ge(r_free, b * NWIN + (NWIN + 1))
                            sp.dma_start(out[bass.ds(b * L, L), :].rearrange("(t p) d -> p t d", p=P),
                                         XN[:, bass.ds(b * TB, TB), :]).then_inc(late_out, 16)
                if stage:
                    break
                sp.wait_ge(xn_taken, B)
                for j in range(3):
                    if j == 2:
                        sp.wait_ge(xt_full, 1)
                    sp.dma_start(XS[:, j % 2, :], xs_dram[j * P:(j + 1) * P, :]).then_inc(xs_in[j % 2], 16)
                with sp.Fori(0, SLOT_TILES // 2) as i:
                    for j in range(2):
                        sp.wait_ge(xt_full, 2 * i + (j + 2))
                        sp.dma_start(XS[:, 1 - j, :], xs_dram[bass.ds(i * (2 * P) + (j + 3) * P, P), :]
                                     ).then_inc(xs_in[1 - j], 16)
                        sp.wait_ge(ys_ready, 2 * i + (j + 2))
                        sp.dma_start(ys_dram[bass.ds(i * (2 * P) + j * P, P), :], YS[j]).then_inc(y_out[j], 16)
                sp.wait_ge(xs_in[0], 16 * (XS_LOADS + 1) // 2)
                sp.sem_inc(phase_done, 1)
                last = SLOT_TILES - 1
                sp.wait_ge(ys_ready, SLOT_TILES + 1)
                sp.dma_start(ys_dram[last * P:(last + 1) * P, :], YS[last % 2]).then_inc(y_out[last % 2], 16)
                sp.wait_ge(y_out[1 - last % 2], 16 * (SLOT_TILES // 2))
                sp.wait_ge(y_out[last % 2], 16 * (last // 2 + 1))
                sp.sem_inc(y_stored, 1)
                sp.wait_ge(phase_done, 5)
                b = LAST_ORDER[0]
                sp.dma_start(XR[:, b * TB:(b + 1) * TB, :], xv[:, b * TB:(b + 1) * TB, :]).then_inc(x_back[0], 16)
            sp.wait_ge(stack_in[0], 2 * NLEV * 16 * (B // 2 + 1))
            sp.wait_ge(xnt_in, 16 * (B + 1))
            sp.wait_ge(late_out, 16 * B // 2)
            sp.wait_ge(out_done, 16 * B // 2)

        @block.gpsimd
        def _(pool):
            made = 0

            def one(ins):
                nonlocal made
                made += 1
                ins.then_inc(consts_made, 1)
                pool.wait_ge(consts_made, made)

            for ident in (IDF, IDB):
                one(pool.memset(ident[:], 0.0))
                one(pool.affine_select(out=ident[:], in_=ident[:], compare_op=ALU.not_equal, fill=1.0, base=0,
                                       pattern=[[-1, P]], channel_multiplier=1))
                if ident is IDF:
                    pool.memset(ZERO, 0.0).then_inc(zero_made, 1)
            one(pool.memset(SEL[:], 0.0))
            for part in range(2):
                one(pool.affine_select(out=SEL[:], in_=SEL[:], compare_op=ALU.not_equal, fill=1.0, base=-HH * part,
                                       pattern=[[-1, HH], [0, P]], channel_multiplier=1))
            one(pool.memset(ONES, 1.0))
            one(pool.affine_select(out=BEFORE, in_=ONES, compare_op=ALU.is_gt, fill=0.0, base=0,
                                   pattern=[[1, P]], channel_multiplier=-1))
            one(pool.memset(VW[:], 1.0))
            one(pool.memset(MH[:], 0.0))
            one(pool.memset(ONE8, 1.0))
            one(pool.memset(RMASK, 1.0))
            one(pool.memset(RMASK.rearrange("p (e t) -> p e t", e=E)[:, :, 0:1], 0.0))
            one(pool.iota(INTS[:, 0:E], [[-1, E]], base=E, channel_multiplier=0))
            one(pool.iota(INTS[:, E:E + NT], [[P, NT]], base=0, channel_multiplier=0))
            one(pool.iota(INTS[:, E + NT:], [[1, XS_TILES]], base=0, channel_multiplier=0))
            assert made == CONSTS

            step = Count()

            def link(ins):
                ins.then_inc(pool_step, 1)
                pool.wait_ge(pool_step, step.add())

            def add_experts(o, v):
                for n in (E // 2, E // 4):
                    link(pool.tensor_tensor(out=v[:, :, 0:n], in0=v[:, :, 0:n], in1=v[:, :, n:2 * n], op=ALU.add))
                link(pool.tensor_tensor(out=o, in0=v[:, :, 0], in1=v[:, :, 1], op=ALU.add))

            pool.wait_ge(bases_ready, 1)
            link(pool.tensor_tensor(out=SLOT, in0=RANK, in1=EXC.rearrange("p (e t) -> p t e", e=E), op=ALU.add))
            link(pool.tensor_tensor(out=SLOT, in0=SLOT, in1=BASE.unsqueeze(1).to_broadcast([P, NT, E]), op=ALU.add))
            for k, one_hot in enumerate((OH1, OH2)):
                link(pool.tensor_tensor(out=PICK, in0=SLOT, in1=one_hot, op=ALU.mult))
                add_experts(SLOTF[:, k, :], PICK)
            link(pool.tensor_copy(IDX[:], SLOTF))
            pool.wait_ge(temps_done, 1)
            pool.sem_inc(temps_done, 1)

            pool.wait_ge(xs_zeroed, 64)
            for b in range(B + 1):
                if b < B:
                    for t in range(TB * b, TB * b + TB):
                        for k in range(2):
                            pool.indirect_dma_start(xs_dram, bass.IndirectOffsetOnAxis(IDX[:, k, t:t + 1], 0),
                                                    XN[:, t, :], None).then_inc(scattered[b], 16)
                if b > 0:
                    pool.wait_ge(scattered[b - 1], 16 * 2 * TB)
                    pool.sem_inc(xn_taken, 1)

            rv = rows_dram.rearrange("(t p) d -> p t d", p=P)
            for b in range(B // 2):
                pool.wait_ge(r_free, (b + 1) * NWIN + 1)
                pool.dma_start(rv[:, b * TB:(b + 1) * TB, :], XN[:, b * TB:(b + 1) * TB, :]).then_inc(rows_out[b // 2], 16)

            with pool.Fori(0, XS_TILES // 2) as i:
                for k in range(2):
                    low_part(pool, 2 * i + k, k, 1)
            pool.wait_ge(low_ready[1], XS_TILES)
            pool.sem_inc(phase_done, 1)

            pool.wait_ge(y_stored, 1)
            pool.wait_ge(phase_done, 5)
            ov = out.rearrange("(t p) d -> p t d", p=P)

            def gather(b, half):
                for t in range(b * TB + half * TB // 2, b * TB + (half + 1) * TB // 2):
                    for k in range(2):
                        pool.indirect_dma_start(YG[:, t, k, :], None, ys_dram,
                                                bass.IndirectOffsetOnAxis(IDX[:, k, t:t + 1], 0)
                                                ).then_inc(gathered[half][b], 16)

            def combine(b, lo, hi):
                rows = slice(b * TB + lo * TB // 2, b * TB + hi * TB // 2)
                n = (hi - lo) * TB // 2
                if b < B // 2:
                    total, first = XN, XN[:, rows, :]
                else:
                    total, first = XR, BOUT[:].unsqueeze(1).to_broadcast([P, n, D])
                link(pool.tensor_tensor(out=total[:, rows, :], in0=XR[:, rows, :], in1=first, op=ALU.add))
                for half in range(lo, hi):
                    pool.wait_ge(gathered[half][b], 16 * TB)
                y = YG[:, rows, :, :]
                weight = PW[:, :, rows].rearrange("p k t -> p t k").unsqueeze(3).to_broadcast([P, n, 2, D])
                link(pool.tensor_tensor(out=y, in0=y, in1=weight, op=ALU.mult))
                for k in range(2):
                    link(pool.tensor_tensor(out=total[:, rows, :], in0=total[:, rows, :], in1=y[:, :, k, :], op=ALU.add))
                if b >= B // 2:
                    pool.sem_inc(rest_ready, hi - lo)

            def gather_batch(b):
                gather(b, 0)
                gather(b, 1)

            xv = x.rearrange("(t p) d -> p t d", p=P)
            first, second = LAST_ORDER[:2]
            gather_batch(first)
            pool.dma_start(XR[:, (first + 1) * TB:, :], xv[:, (first + 1) * TB:, :]).then_inc(x_back[1], 16)
            pool.wait_ge(x_back[0], 16)
            combine(first, 0, 1)
            gather(second, 0)
            combine(first, 1, 2)
            gather(second, 1)
            pool.dma_start(XR[:, 0:NT // 2, :], xv[:, 0:NT // 2, :]).then_inc(x_back[2], 16)
            gather_batch(LAST_ORDER[2])
            pool.dma_start(XN[:, 0:NT // 2, :], rv).then_inc(rows_back, 16)
            pool.wait_ge(x_back[1], 16)
            combine(second, 0, 2)
            pool.wait_ge(x_back[2], 16)
            pool.wait_ge(rows_back, 16)
            for i in range(2, B):
                if i < B - 1:
                    gather_batch(LAST_ORDER[i + 1])
                b = LAST_ORDER[i]
                combine(b, 0, 2)
                if b < B // 2:
                    pool.dma_start(ov[:, b * TB:(b + 1) * TB, :], XN[:, b * TB:(b + 1) * TB, :]).then_inc(out_done, 16)

        @block.scalar
        def _(act):
            c = pair_counts()
            act.dma_start(GW, gate).then_inc(gate_in, 16)
            act.dma_start(WQKV[:], wqkv).then_inc(consts_in, 16)
            act.dma_start(BQK[:], bqk).then_inc(consts_in, 16)
            act.dma_start(BV, bv).then_inc(consts_in, 16)
            act.dma_start(WOUT[:], wout).then_inc(consts_in, 16)
            act.dma_start(BOUT[:], bout).then_inc(consts_in, 16)
            act.sem_inc(probs_ready, 2)
            act.sem_inc(ht_free, 1)

            def take_sqrt(g):
                act.wait_ge(var_ready, g + 1)
                act.activation(STD[:, 8 * g:8 * g + 8], VAR[:, 8 * g:8 * g + 8], ACT.Sqrt).then_inc(std_ready, 1)

            def take_part(blk, bk, full, n):
                if blk == 0:
                    wait_some(act, parts_out, c["NB"].now() * PARTS_OUT)
                    c["NB"].add()
                act.wait_ge(full, n)
                act.activation(PARTS[:, 0, blk, :], bk[:, 0:SPAN], ACT.Identity,
                               bias=BQK[:, blk:blk + 1]).then_inc(part0_ready, 1)

            take_sqrt(0)
            take_sqrt(1)
            for i in range(NT // 2):
                act.wait_ge(tok_full, i + 1)
                act.activation(XT[:, :, 2 * i * P:2 * (i + 1) * P],
                               TOK_BANK[i % 2].rearrange("p (c n) -> p c n", c=NC_D), ACT.Copy).then_inc(tok_free, 1)
                if i in (3, 7):
                    take_sqrt((i + 1) // 4 + 1)
                if i == FIRST_STEP:
                    act.wait_ge(consts_in, 80)
                    for blk in range(4):
                        take_part(blk, FIRST_BANK[blk], first_full, blk + 1)
                if i % 2 == 0 and i:
                    src = i // 2 - 1
                    act.wait_ge(tok_free, i)
                    for nb in (src, src + B):
                        if 0 < nb < B + 2:
                            act.dma_start(xt_dram[nb], XT[:, :, src * L:src * L + SPAN]).then_inc(xt_out, 16)
            act.wait_ge(tok_free, NT // 2)
            act.dma_start(xt_dram[B - 1], XT[:, :, (B - 1) * L:(B - 1) * L + SPAN]).then_inc(xt_out, 16)
            act.wait_ge(gap_ready, 2)
            act.activation(E2, PA, ACT.Exp).then_inc(e2_ready, 1)
            c["T"].add(1)

            def exps(u, q):
                act.wait_ge(st_full, c["ST"].add())
                act.activation(PT[:, 2 * (u % 2) + q, :], ST_BANK[q], ACT.Exp, scale=SCALE).then_inc(probs_ready, 1)

            def take_turned():
                act.wait_ge(t_full, c["T"].add())
                act.activation(OTS[:], T_BANK[:, 0:D].rearrange("p (c n) -> p c n", c=NC_D), ACT.Copy
                               ).then_inc(t_free, 1)

            def pair(stage):
                for par in range(2):
                    for u in range(UNITS):
                        if stage and u == 3:
                            act.wait_ge(y_stored, 1)
                        if u % 2 == 1 and u > 1:
                            take_turned()
                        if u > 0:
                            exps(u, 1)
                        c["T"].add(1)
                        if u < 4:
                            take_part(u, W_BANK, w_full, c["W"].add())
                        else:
                            c["W"].add(1)
                        if u < UNITS - 1:
                            exps(u + 1, 0)
                    exps(0, 0)
                    take_turned()
                    exps(0, 1)

            exps(0, 0)
            exps(0, 1)
            for stage in range(2):
                with loop(act, PAIRS, c["T"], c["W"], c["ST"], c["NB"]):
                    pair(stage)
                if stage:
                    break
                def high_part(j, k, half, used=None):
                    weights = weights_of(act, j, half)
                    if used is not None:
                        act.wait_ge((h1_full, h2_full)[half], used)
                    act.activation(WS[:, 1 - k, half, 0], weights, ACT.Copy
                                   ).then_inc(high_ready[half], 1)

                act.wait_ge(temps_done, 2)
                act.wait_ge(weights_in, 16 * E)
                act.wait_ge(xn_taken, B)
                high_part(0, 0, 0)
                high_part(0, 0, 1)
                act.wait_ge(probs_ready, c["ST"].now() + 2)

                def take_tanh(j, k):
                    act.wait_ge(h1_full, j + 1)
                    act.activation(HID[:, k, :], bank(2 * k), ACT.Tanh, scale=0.5).then_inc(tanh_ready, 1)

                def take_ht(j):
                    act.wait_ge(ht_full, j + 1)
                    act.activation(HTS, bank(6).rearrange("p (c n) -> p c n", c=FC), ACT.Copy).then_inc(ht_free, 1)

                def take_xt(j, k):
                    act.wait_ge(xt_full, j + 1)
                    act.activation(XTS[:, k, 0], bank(4 + k)[:, 0:D].rearrange("p (c n) -> p c n", c=NC_D),
                                   ACT.Copy).then_inc(xt_high, 1)

                take_xt(0, 0)
                take_xt(1, 1)
                act.wait_ge(rows_out[0], 32)
                high_part(1, 1, 0)
                take_tanh(0, 0)
                act.wait_ge(rows_out[1], 32)
                high_part(1, 1, 1)
                with act.Fori(0, SLOT_TILES // 2) as i:
                    for k in range(2):
                        j = 2 * i + k
                        high_part(j + 2, k, 0, j + 1)
                        take_tanh(j + 1, 1 - k)
                        take_ht(j)
                        high_part(j + 2, k, 1, j + 1)
                        take_xt(j + 2, k)
                take_ht(SLOT_TILES - 1)
                act.wait_ge(ht_free, SLOT_TILES + 1)
                act.wait_ge(high_ready[1], XS_TILES)
                act.sem_inc(phase_done, 1)
                act.wait_ge(phase_done, 5)

        @block.vector
        def _(dve):
            c = pair_counts()
            step = Count(0, 0)

            def link(ins):
                ins.then_inc(dve_step, 1)
                dve.wait_ge(dve_step, step.add())

            def tt(o, a, b, op):
                return dve.tensor_tensor(out=o, in0=a, in1=b, op=op)

            def ts(o, a, s1, s2, op0, op1):
                return dve.tensor_scalar(out=o, in0=a, scalar1=s1, scalar2=s2, op0=op0, op1=op1)

            def red(o, a, op, **kw):
                return dve.tensor_reduce(out=o, in_=a, axis=AX_X, op=op, **kw)

            def wide(v, n=E):
                return v.unsqueeze(2).to_broadcast([P, v.shape[1], n])

            for s in (o_free, r_free, w_free, ys_ready):
                dve.sem_inc(s, 1)
            dve.sem_inc(g_done, 2)
            dve.sem_inc(hid_done, 2)
            dve.sem_inc(xt_free, 2)

            def variance(g):
                lo, hi = 8 * g, 8 * g + 8
                dve.wait_ge(x_in[g], 16)
                for t in range(lo, hi):
                    dve.bn_stats(out=STAT[:, t, :], in_=XN[:, t, :]).then_inc(dve_step, 1)
                    step.add()
                dve.wait_ge(dve_step, step.now())
                me, mo = STAT[:, lo:hi, 1], STAT[:, lo:hi, 4]
                ve, vo = STAT[:, lo:hi, 2], STAT[:, lo:hi, 5]
                mean, var, dif, tmp = MEAN[:, lo:hi], VAR[:, lo:hi], DIF[:, lo:hi], TMP[:, lo:hi]
                tt(tmp, ve, vo, ALU.add).then_inc(dve_step, 1)
                step.add()
                tt(mean, me, mo, ALU.add).then_inc(dve_step, 1)
                step.add()
                link(tt(dif, me, mo, ALU.subtract))
                ts(mean, mean, 0.5, None, ALU.mult, ALU.bypass).then_inc(dve_step, 1)
                step.add()
                link(tt(dif, dif, dif, ALU.mult))
                link(ts(dif, dif, 0.25, EPS, ALU.mult, ALU.add))
                link(dve.scalar_tensor_tensor(out=var, in0=tmp, scalar=1.0 / D, in1=dif, op0=ALU.mult, op1=ALU.add))
                dve.sem_inc(var_ready, 1)

            def normalise(g):
                lo, hi = 8 * g, 8 * g + 8
                rs, var, tmp = RS[:, lo:hi], VAR[:, lo:hi], TMP[:, lo:hi]
                dve.wait_ge(std_ready, g + 1)
                link(dve.reciprocal(out=rs, in_=STD[:, lo:hi]))
                link(tt(tmp, rs, rs, ALU.mult))
                link(tt(tmp, tmp, var, ALU.mult))
                link(ts(tmp, tmp, -0.5, 1.5, ALU.mult, ALU.add))
                link(tt(rs, rs, tmp, ALU.mult))
                for t in range(lo, hi):
                    ts(XN[:, t, :], XN[:, t, :], MEAN[:, t:t + 1], RS[:, t:t + 1], ALU.subtract, ALU.mult
                       ).then_inc(xn_ready, 1)

            variance(0)
            for g in range(4):
                if g < 3:
                    variance(g + 1)
                normalise(g)

            dve.wait_ge(consts_made, CONSTS)
            dve.tensor_copy(REV, INTS[:, 0:E])
            dve.tensor_copy(TH, INTS[:, E:E + NT])
            link(dve.tensor_copy(JI, INTS[:, E + NT:]))
            dve.wait_ge(consts_in, 80)
            for k in range(NC_D):
                dve.tensor_copy(BVB[:, k, :], BV[:, k:k + 1].to_broadcast([P, P])).then_inc(bv_ready, 1)

            def split(blk, first=False):
                wait_some(dve, parts_ready, c["QK"].now())
                dve.wait_ge(part0_ready, c["QK"].add())
                dve.wait_ge(*((first_full, blk + 1) if first else (w_full, c["W"].add())))
                bk = FIRST_BANK[blk] if first else W_BANK
                rest = dve.scalar_tensor_tensor(out=REST, in0=bk[:, 0:SPAN], scalar=BQK[:, blk:blk + 1],
                                                in1=PARTS[:, 0, blk, :], op0=ALU.add, op1=ALU.subtract)
                if first:
                    link(rest)
                else:
                    rest.then_inc(w_free, 1)
                    dve.wait_ge(w_free, c["W"].now() + 1)
                link(dve.tensor_copy(PARTS[:, 1, blk, :], REST))
                tt(PARTS[:, 2, blk, :], REST, PARTS[:, 1, blk, :], ALU.subtract).then_inc(parts_ready, 1)

            def take_values(n):
                dve.wait_ge(w_full, c["W"].add())
                dve.tensor_copy(VW[:, n, :, 0:HD], W_BANK[:, 0:D].rearrange("p (h d) -> p h d", d=HD)
                                ).then_inc(w_free, 1)

            def route(half):
                ts_ = slice(half * HALF, (half + 1) * HALF)

                def top(scores, most, one_hot):
                    link(red(most, scores, ALU.max))
                    link(tt(EQ[:, ts_, :], scores, wide(most), ALU.is_equal))
                    link(tt(KEY[:, ts_, :], EQ[:, ts_, :], REV.unsqueeze(1).to_broadcast([P, HALF, E]), ALU.mult))
                    link(red(KM[:, ts_], KEY[:, ts_, :], ALU.max))
                    link(tt(one_hot, KEY[:, ts_, :], wide(KM[:, ts_]), ALU.is_equal))

                g, g2, oh1, oh2 = (v[:, ts_, :] for v in (G, G2, OH1, OH2))
                dve.wait_ge(gates_full, half + 1)
                link(dve.tensor_copy(g, bank(half)[:, 0:HALF * E].rearrange("p (t e) -> p t e", e=E)))
                top(g, M1[:, ts_], oh1)
                link(dve.scalar_tensor_tensor(out=g2, in0=oh1, scalar=FAR, in1=g, op0=ALU.mult, op1=ALU.add))
                top(g2, M2[:, ts_], oh2)
                tt(MASK[:, ts_, :], oh1, oh2, ALU.add).then_inc(mask_ready, 1)
                tt(PA[:, ts_], M2[:, ts_], M1[:, ts_], ALU.subtract).then_inc(gap_ready, 1)

            for blk in range(4):
                split(blk, True)
            route(0)
            route(1)

            dve.wait_ge(first_full, 4 + NWIN)
            for n in range(0, NWIN, 2):
                dve.tensor_copy(VW[:, n:n + 2, :, 0:HD], TOK_BANK[n // 2].rearrange("p (n h d) -> p n h d", n=2, d=HD)
                                ).then_inc(values_taken, 1)
            dve.wait_ge(bv_full, 1)
            link(tt(BOUT[:], BOUT[:], BV_BANK, ALU.add))

            dve.wait_ge(ranks_full, 1)
            ps_rank = bank(0)[:, 0:NT * E].rearrange("p (t e) -> p t e", e=E)
            ps_tot = bank(0)[:, NT * E:2 * NT * E].rearrange("p (t e) -> p e t", e=E)
            tot, inc = (v.rearrange("p (e t) -> p e t", e=E) for v in (TOT, INC))
            link(dve.tensor_copy(RANK, ps_rank))
            link(dve.tensor_copy(tot, ps_tot))
            dve.sem_inc(ranks_taken, 1)
            dve.wait_ge(e2_ready, 1)
            link(ts(M1, E2, 1.0, None, ALU.add, ALU.bypass))
            link(dve.reciprocal(out=M2, in_=M1))
            link(ts(PW[:, 0, :], M2, 0.5, None, ALU.mult, ALU.bypass))
            link(dve.scalar_tensor_tensor(out=PW[:, 1, :], in0=E2, scalar=0.5, in1=M2, op0=ALU.mult, op1=ALU.mult))
            link(dve.tensor_tensor_scan(out=INC, data0=RMASK, data1=TOT, initial=0.0, op0=ALU.mult, op1=ALU.add))
            link(tt(EXC, INC, TOT, ALU.subtract))

            def take_max():
                wait_some(dve, mh_ready, c["S"].now())
                dve.wait_ge(s_full, c["S"].add())
                red(MNEG[:], S_BANKS.rearrange("p (h k) -> p h k", k=WIN), ALU.max, negate=True).then_inc(s_free, 1)
                dve.wait_ge(s_free, c["S"].now())
                link(dve.tensor_copy(MH[:, 0:HH], MNEG[:]))
                tt(MH[:, HH:2 * HH], MNEG[:], MH[:, 0:HH], ALU.subtract).then_inc(mh_ready, 1)

            def take_negm(k):
                dve.wait_ge(t_full, c["T"].add())
                dve.tensor_copy(NEGM[:, k, :], T_BANK[0:STK, 0:P // 2].bitcast(BF16)).then_inc(t_free, 1)

            take_max()
            take_negm(0)
            take_max()
            link(tt(CMP, inc[:, :, NT - 1:NT].to_broadcast([P, E, NT]), TH.unsqueeze(1).to_broadcast([P, E, NT]),
                    ALU.is_gt))
            link(red(NTL, CMP, ALU.add))
            link(dve.tensor_tensor_scan(out=INCT, data0=ONE8, data1=NTL, initial=0.0, op0=ALU.mult, op1=ALU.add))
            link(tt(BASE, INCT, NTL, ALU.subtract))
            link(ts(BASE, BASE, float(P), None, ALU.mult, ALU.bypass))
            dve.sem_inc(bases_ready, 1)
            link(tt(CMPJ, INCT.unsqueeze(1).to_broadcast([P, XS_TILES, E]), wide(JI), ALU.is_le))
            link(red(EJF, CMPJ, ALU.add))
            link(ts(EJF, EJF, float(E - 1), None, ALU.min, ALU.bypass))
            link(dve.tensor_copy(EJ[:], EJF[0:1, :]))
            dve.sem_inc(temps_done, 1)

            def norm():
                dve.wait_ge(o_free, c["O"].now() + 1)
                dve.wait_ge(o_full, c["O"].add())
                o = O_BANK[:, 0:H * (HD + 1)].rearrange("p (h d) -> p h d", d=HD + 1)
                link(dve.reciprocal(out=RDEN[:], in_=o[:, :, HD]))
                tt(OSB[:], o[:, :, 0:HD], RDEN[:].unsqueeze(2).to_broadcast([P, H, HD]), ALU.mult
                   ).then_inc(o_free, 1)

            def row(t, of=XN):
                return of[:, bass.ds(t, 1), :].rearrange("p o d -> p (o d)")

            def project(stage, b, n):
                dve.wait_ge(r_full, c["R"].add())
                rest = row(b * TB + n, XR) if stage else BOUT[:]
                tt(row(b * TB + n), R_BANK[:, 0:D], rest, ALU.add).then_inc(r_free, 1)

            for stage in range(2):
                step.per = PAIR_STEPS
                with loop(dve, PAIRS, step, c["T"], c["W"], c["S"], c["O"], c["R"], c["QK"]) as i:
                    for par in range(2):
                        b = 4 * stage + 2 * i + par
                        for u in range(UNITS):
                            if u % 2 == 1 and u > 1:
                                c["T"].add(1)
                            if stage and u == 2:
                                dve.wait_ge(y_stored, 1)
                            take_negm((u + 1) % 2)
                            if u < 4:
                                split(u)
                            elif u < 6:
                                take_values(u - 4)
                            if u in (2, 4, 6):
                                norm()
                            if u == 6:
                                take_values(2)
                            take_max()
                            if u == 3:
                                dve.wait_ge(xn_taken, b + 1)
                            if stage and u in (3, 7):
                                dve.wait_ge(rest_ready, 2 * (2 * i + par) + (1 if u == 3 else 2))
                            if u % 2 == 1 and u > 1:
                                project(stage, b, u // 2 - 1)
                        norm()
                        take_values(3)
                        c["T"].add(1)
                        project(stage, b, NWIN - 1)
                if stage:
                    break
                low_part(dve, 0, 0, 0)
                dve.wait_ge(r_free, c["R"].now() + 1)

                def hidden(j, k):
                    dve.wait_ge(tanh_ready, j + 1)
                    dve.scalar_tensor_tensor(out=HID[:, k, :], in0=HID[:, k, :], scalar=1.0, in1=bank(2 * k),
                                             op0=ALU.add, op1=ALU.mult).then_inc(g_done, 1)
                    dve.wait_ge(g_done, j + 3)
                    dve.wait_ge(h2_full, j + 1)
                    tt(HID[:, k, :], HID[:, k, :], bank(2 * k + 1), ALU.mult).then_inc(hid_done, 1)

                def take_y(j, k, stored):
                    dve.wait_ge(y_full, j + 1)
                    wait_some(dve, y_out[k], 16 * stored)
                    dve.tensor_copy(YS[k], bank(7)[:, 0:D]).then_inc(ys_ready, 1)

                def low_xt(j, k):
                    dve.wait_ge(xt_high, j + 1)
                    tt(XTS[:, k, 1], bank(4 + k)[:, 0:D].rearrange("p (c n) -> p c n", c=NC_D),
                       XTS[:, k, 0].bitcast(F32), ALU.subtract).then_inc(xt_free, 1)

                low_xt(0, 0)
                low_xt(1, 1)
                low_part(dve, 1, 1, 0)
                hidden(0, 0)
                for k in range(2):
                    low_part(dve, k + 2, k, 0)
                    hidden(k + 1, 1 - k)
                    low_xt(k + 2, k)
                    take_y(k, k, 0)
                with dve.Fori(1, SLOT_TILES // 2) as i:
                    for k in range(2):
                        low_part(dve, 2 * i + k + 2, k, 0)
                        hidden(2 * i + k + 1, 1 - k)
                        low_xt(2 * i + k + 2, k)
                        take_y(2 * i + k, k, i)
                take_y(SLOT_TILES - 1, (SLOT_TILES - 1) % 2, SLOT_TILES // 2)
                dve.wait_ge(ys_ready, SLOT_TILES)
                dve.sem_inc(phase_done, 1)
                dve.wait_ge(phase_done, 5)

        @block.tensor
        def _(pe):
            c = pair_counts()

            def mm(o, a, b, start=True, stop=True):
                return pe.matmul(o, a, b, start=start, stop=stop)

            def project_block(o, blk, xt, full):
                for ch in range(NC_D):
                    last = mm(o, WQKV[:, ch, blk * P:(blk + 1) * P], xt[:, ch, 0:SPAN], ch == 0, ch == NC_D - 1)
                last.then_inc(full, 1)

            def project_values(o, n, xt, full):
                for ch in range(NC_D):
                    last = mm(o, xt[:, ch, n * STRIDE:n * STRIDE + WIN], WQKV[:, ch, 2 * D:3 * D],
                              ch == 0, ch == NC_D - 1)
                last.then_inc(full, 1)

            pe.wait_ge(consts_made, 2)

            def turn_pair(i):
                pe.wait_ge(xn_ready, 2 * i + 2)
                if i > 1:
                    pe.wait_ge(tok_free, i - 1)
                for ch in range(NC_D):
                    for k in range(2):
                        last = pe.transpose(TOK_BANK[i % 2][:, (2 * ch + k) * P:(2 * ch + k + 1) * P],
                                            XN[:, 2 * i + k, ch * P:(ch + 1) * P], IDF[:])
                last.then_inc(tok_full, 1)

            def score_pair(i):
                pe.wait_ge(tok_free, i + 1)
                for t in (2 * i, 2 * i + 1):
                    for ch in range(NC_D):
                        last = mm(bank(t // HALF)[:, (t % HALF) * E:(t % HALF + 1) * E], XT[:, ch, t * P:(t + 1) * P], GW[:, ch, :],
                                  ch == 0, ch == NC_D - 1)
                return last

            turn_pair(0)
            pe.wait_ge(gate_in, 16)
            for i in range(1, NT // 2):
                turn_pair(i)
                last = score_pair(i - 1)
                if i == HALF // 2:
                    last.then_inc(gates_full, 1)
                if i == FIRST_STEP:
                    pe.wait_ge(consts_in, 80)
                    for blk in range(4):
                        project_block(FIRST_BANK[blk][:, 0:SPAN], blk, XT, first_full)
            pe.wait_ge(bv_ready, NC_D)
            for ch in range(NC_D):
                last = mm(BV_BANK, BVB[:, ch, :], WOUT[:, ch, :], ch == 0, ch == NC_D - 1)
            last.then_inc(bv_full, 1)
            score_pair(NT // 2 - 1).then_inc(gates_full, 1)
            for n in range(NWIN):
                project_values(TOK_BANK[n // 2][:, (n % 2) * D:(n % 2 + 1) * D], n, XT, first_full)

            def queries_keys(blk):
                pe.wait_ge(w_free, c["W"].now() + 1)
                project_block(W_BANK[:, 0:SPAN], blk, XNT, w_full)
                c["W"].add()

            def values(n):
                pe.wait_ge(w_free, c["W"].now() + 1)
                project_values(W_BANK[:, 0:D], n, XNT, w_full)
                c["W"].add()

            pe.wait_ge(consts_made, CONSTS)
            pe.wait_ge(mask_ready, 2)
            mm(bank(0)[:, 0:NT * E], BEFORE, MASK.rearrange("p t e -> p (t e)"))
            mm(bank(0)[:, NT * E:2 * NT * E], ONES, MASK.rearrange("p t e -> p (t e)")).then_inc(ranks_full, 1)

            def scores(par, u):
                n, half = u // 2, u % 2
                wait_some(pe, s_free, c["S"].now())
                w = slice(n * STRIDE, n * STRIDE + WIN)
                for h in range(HH):
                    last = mm(S_BANKS[:, h * WIN:(h + 1) * WIN], QS[:, par, half * HH + h, w],
                              KS[:, par, half * HH + h, w])
                last.then_inc(s_full, 1)
                c["S"].add()

            def shift_row():
                pe.wait_ge(mh_ready, c["S"].now())
                wait_some(pe, t_free, c["T"].now())
                pe.transpose(T_BANK[0:STK, 0:P // 2].bitcast(BF16), MH[:], IDB[:]).then_inc(t_full, 1)
                c["T"].add()

            def shifted(par, u):
                n, half = u // 2, u % 2
                w = slice(n * STRIDE, n * STRIDE + WIN)
                pe.wait_ge(t_free, c["T"].now())
                for q in range(2):
                    pe.wait_ge(probs_ready, c["ST"].now() + 1)
                    for hq in range(HQ):
                        h = q * HQ + hq
                        o = ST_BANK[q][:, hq * WIN:(hq + 1) * WIN]
                        mm(o, KS[:, par, half * HH + h, w], QS[:, par, half * HH + h, w], True, False)
                        last = mm(o, SEL[:, h, :], NEGM[:, u % 2, :], False, True)
                    last.then_inc(st_full, 1)
                    c["ST"].add()

            def weighted(u, behind):
                n, half = u // 2, u % 2
                if half == 0:
                    pe.wait_ge(o_free, c["O"].now() + 1)
                pe.wait_ge(probs_ready, c["ST"].now() + 2 - behind)
                for h in range(HH):
                    hh = half * HH + h
                    last = mm(O_BANK[:, hh * (HD + 1):(hh + 1) * (HD + 1)],
                              PT[:, 2 * (u % 2) + h // HQ, (h % HQ) * WIN:(h % HQ + 1) * WIN], VW[:, n, hh, :])
                if half:
                    last.then_inc(o_full, 1)
                    c["O"].add()

            def turn():
                pe.wait_ge(o_free, c["O"].now() + 1)
                pe.wait_ge(t_free, c["T"].now())
                for ch in range(NC_D):
                    last = pe.transpose(T_BANK[:, ch * P:(ch + 1) * P],
                                        OSB[:].rearrange("p h d -> p (h d)")[:, ch * P:(ch + 1) * P], IDF[:])
                last.then_inc(t_full, 1)
                c["T"].add()

            def project(tfree):
                pe.wait_ge(t_free, tfree)
                pe.wait_ge(r_free, c["R"].now() + 1)
                for ch in range(NC_D):
                    last = mm(R_BANK[:, 0:D], OTS[:, ch, :], WOUT[:, ch, :], ch == 0, ch == NC_D - 1)
                last.then_inc(r_full, 1)
                c["R"].add()

            pe.wait_ge(stack_in[0], 2 * NLEV * 16)
            pe.wait_ge(ranks_taken, 1)
            pe.wait_ge(values_taken, NWIN // 2)
            scores(0, 0)
            shift_row()
            scores(0, 1)
            shifted(0, 0)
            loads = Count(2 * NLEV * 16, 2 * NLEV * 16)

            for stage in range(2):
                with loop(pe, PAIRS, c["T"], c["W"], c["S"], c["ST"], c["O"], c["R"], loads) as i:
                    for par in range(2):
                        b = 2 * i + (4 * stage + par)
                        for u in range(UNITS):
                            if u % 2 == 1 and u > 1:
                                turn()
                            if u == 0:
                                pe.wait_ge(xnt_in, b * 16 + 16)
                            if u < 4:
                                queries_keys(u)
                            else:
                                values(u - 4)
                            if u in (1, UNITS - 1):
                                weighted(u - 1, 2)
                            shift_row()
                            if 1 < u < UNITS - 1:
                                weighted(u - 1, 2)
                            if u < UNITS - 2:
                                scores(par, u + 2)
                            else:
                                if u == UNITS - 2:
                                    if par == 1:
                                        loads.add(2 * NLEV * 16)
                                    pe.wait_ge(stack_in[1 - par], loads.now())
                                scores(1 - par, u + 2 - UNITS)
                            if u < UNITS - 1:
                                shifted(par, u + 1)
                            if u % 2 == 1 and u > 1:
                                project(c["T"].now(1))
                        weighted(UNITS - 1, 0)
                        shifted(1 - par, 0)
                        turn()
                        project(c["T"].now())
                if stage:
                    break
                pe.wait_ge(r_full, c["R"].now())
                pe.wait_ge(o_free, c["O"].now() + 1)
                pe.wait_ge(t_free, c["T"].now())
                pe.wait_ge(w_free, c["W"].now() + 1)
                pe.wait_ge(s_free, c["S"].now())
                pe.wait_ge(probs_ready, c["ST"].now() + 2)
                pe.wait_ge(weights_in, 16 * E)
                pe.wait_ge(temps_done, 2)

                def tokens(j, k):
                    pe.wait_ge(xs_in[k], (j - k) * 8 + 16)
                    pe.wait_ge(xt_free, j + 1)
                    for ch in range(NC_D):
                        last = pe.transpose(bank(4 + k)[:, ch * P:(ch + 1) * P], XS[:, k, ch * P:(ch + 1) * P], IDF[:])
                    last.then_inc(xt_full, 1)

                def up(j, k, half):
                    full, free = ((h1_full, g_done), (h2_full, hid_done))[half]
                    if half == 0:
                        pe.wait_ge(xt_free, j + 3)
                    pe.wait_ge(low_ready[half], j + 1)
                    pe.wait_ge(free, j + 1)
                    n = 0
                    for ch in range(NC_D):
                        for lx, lw in ((0, 0), (0, 1), (1, 0)):
                            last = mm(bank(2 * k + half), XTS[:, k, lx, ch, :],
                                      WS[:, 1 - k, half, lw, ch, :], n == 0, n == 3 * NC_D - 1)
                            n += 1
                    last.then_inc(full, 1)

                def turn_hidden(j, k):
                    pe.wait_ge(hid_done, j + 3)
                    pe.wait_ge(ht_free, j + 1)
                    for f in range(FC):
                        last = pe.transpose(bank(6)[:, f * P:(f + 1) * P], HID[:, k, f * P:(f + 1) * P], IDF[:])
                    last.then_inc(ht_full, 1)

                def down(j, at):
                    pe.wait_ge(ht_free, j + 2)
                    pe.wait_ge(ys_ready, j + 1)
                    for f in range(FC):
                        last = mm(bank(7)[:, 0:D], HTS[:, f, :],
                                  WALL[:, bass.ds(at + 2 * NC_D * FH + f * D, D)], f == 0, f == FC - 1)
                    last.then_inc(y_full, 1)

                def expert(j):
                    return pe.value_load(EJ[0:1, bass.ds(j, 1)], min_val=0, max_val=E - 1) * WE

                tokens(0, 0)
                tokens(1, 1)
                up(0, 0, 0)
                up(0, 0, 1)
                pe.wait_ge(r_free, c["R"].now() + 1)
                with pe.Fori(0, SLOT_TILES // 2) as i:
                    for k in range(2):
                        j = 2 * i + k
                        up(j + 1, 1 - k, 0)
                        at = expert(j)
                        turn_hidden(j, k)
                        up(j + 1, 1 - k, 1)
                        tokens(j + 2, k)
                        down(j, at)
                j = SLOT_TILES - 1
                turn_hidden(j, j % 2)
                down(j, expert(j))
                pe.wait_ge(y_full, SLOT_TILES)
                pe.sem_inc(phase_done, 1)
                pe.wait_ge(phase_done, 5)


_NAMES = ("L0_attn_x", "L0_attn_w_qkv", "L0_attn_b_qkv", "L0_attn_w_out", "L0_attn_b_out", "L0_ffn_w12", "L0_ffn_w3",
          "L0_ffn_gate_w")


def kernel(**inputs):
    import numpy as np
    import concourse.bacc as bacc
    from concourse.bass_utils import run_bass_kernel_spmd

    x, w_qkv, b_qkv, w_out, b_out, w12, w3, gate_w = (np.asarray(inputs[n]) for n in _NAMES)

    def down(w):
        return w.reshape(-1, P, w.shape[-1]).transpose(1, 0, 2).reshape(P, -1)

    w12_t = w12.transpose(0, 2, 1).reshape(E, NC_D, P, 2 * FH).transpose(2, 0, 1, 3).reshape(P, E, -1)
    w3_t = w3.transpose(0, 2, 1).reshape(E, FC, P, D).transpose(2, 0, 1, 3).reshape(P, E, -1)
    arrays = {
        "x": x.reshape(B * L, D),
        "wqkv": down(w_qkv),
        "bqk": b_qkv[:2 * D].reshape(4, P).T,
        "bv": b_qkv[2 * D:].reshape(NC_D, P).T,
        "wout": down(w_out),
        "bout": np.broadcast_to(b_out, (P, D)),
        "gate": down(gate_w.T),
        "wexp": np.concatenate([w12_t, w3_t], axis=2).reshape(P, E * WE),
    }
    arrays = {f"in_{k}": np.ascontiguousarray(v) for k, v in arrays.items()}
    nc = bacc.Bacc("TRN2", target_bir_lowering=False, num_devices=1)
    args = [nc.dram_tensor(k, v.shape, mybir.dt.from_np(v.dtype), kind="ExternalInput").ap()
            for k, v in arrays.items()]
    args.append(nc.dram_tensor("out_0", (B * L, D), F32, kind="ExternalOutput").ap())
    layer(nc, *args)
    r = run_bass_kernel_spmd(nc, [arrays], core_ids=[0])
    return r.results[0]["out_0"].reshape(B, L, D)
```
